# Optimizing a Trainium2 kernel written in Bass

```python
import numpy as np
import jax
import jax.numpy as jnp

def _softmax(x, axis=-1):
    return jax.nn.softmax(x, axis=axis)

def _gelu(x):
    return jax.nn.gelu(x, approximate=True)

def _silu(x):
    return jax.nn.silu(x)

def _sigmoid(x):
    return jax.nn.sigmoid(x)

def _layernorm(x, axis=-1, eps=1e-05):
    m = jnp.mean(x, axis=axis, keepdims=True)
    v = jnp.var(x, axis=axis, keepdims=True)
    return (x - m) / jnp.sqrt(v + eps)

def _scatter_add(tgt, idx, src, axis=0):
    return tgt.at[idx].add(src)

def _segment_sum(src, seg, n):
    return jax.ops.segment_sum(src, seg, n)
kernel_name = 'mk_adaln_d1_jaxref_r8_888ff4'

def setup_inputs(seed: int=0):
    np.random.seed(seed)
    _w = jnp.asarray

    def _L0_attn_setup():
        import jax, jax.numpy as jnp
        import numpy as np
        RMS_EPS = 1e-06
        ROPE_BASE = 10000.0
        WINDOW = 64
        N_HEADS = 16
        N_KV_HEADS = 4

        def _rope_cos_sin(seq_len, head_dim, dtype):
            inv_freq = 1.0 / ROPE_BASE ** (jnp.arange(0, head_dim, 2, dtype=jnp.float32) / head_dim)
            ang = jnp.arange(seq_len, dtype=jnp.float32)[:, None] * inv_freq[None, :]
            return (jnp.cos(ang).astype(dtype), jnp.sin(ang).astype(dtype))

        def _apply_rope(x, cos, sin):
            B, S, H, hd = x.shape
            xr = x.reshape(B, S, H, hd // 2, 2)
            x1, x2 = (xr[..., 0], xr[..., 1])
            c = cos[None, :, None, :]
            s = sin[None, :, None, :]
            o1 = x1 * c - x2 * s
            o2 = x1 * s + x2 * c
            return jnp.stack([o1, o2], axis=-1).reshape(B, S, H, hd)
        key = jax.random.key(seed)
        ks = jax.random.split(key, 6)
        B, S, D = (2, 256, 256)
        hd = D // N_HEADS
        kv_dim = N_KV_HEADS * hd
        sc = lambda fan_in: 1.0 / np.sqrt(fan_in)
        return {'x': jax.random.normal(ks[0], (B, S, D), jnp.float32), 'rms_w': jnp.ones((D,), jnp.float32), 'wq': jax.random.normal(ks[1], (D, D), jnp.float32) * sc(D), 'wk': jax.random.normal(ks[2], (D, kv_dim), jnp.float32) * sc(D), 'wv': jax.random.normal(ks[3], (D, kv_dim), jnp.float32) * sc(D), 'wo': jax.random.normal(ks[4], (D, D), jnp.float32) * sc(D)}
    _L0_attn_in = _L0_attn_setup()

    def _L0_ffn_setup():
        import jax, jax.numpy as jnp
        import numpy as np
        N_EXPERTS = 16
        TOP_K = 4
        N_GROUP = 4
        TOPK_GROUP = 2
        NORM_TOPK = True
        ROUTED_SCALE = 2.5
        H = 256
        F_MOE = 128
        F_SHARED = 256
        B, S = (2, 256)

        def _route(hidden, gate_weight, bias):
            T = hidden.shape[0]
            epg = N_EXPERTS // N_GROUP
            logits = hidden @ gate_weight.T
            scores = jax.nn.sigmoid(logits)
            scores_for_choice = scores + bias[None, :]
            grp = scores_for_choice.reshape(T, N_GROUP, epg)
            group_scores = jax.lax.top_k(grp, 2)[0].sum(-1)
            group_idx = jax.lax.top_k(group_scores, TOPK_GROUP)[1]
            group_mask = jax.nn.one_hot(group_idx, N_GROUP, dtype=jnp.bool_).any(1)
            score_mask = jnp.repeat(group_mask, epg, axis=-1)
            masked = jnp.where(score_mask, scores_for_choice, -jnp.inf)
            topk_idx = jax.lax.top_k(masked, TOP_K)[1]
            topk_weight = jnp.take_along_axis(scores, topk_idx, axis=1)
            return (topk_weight, topk_idx)

        def _swiglu(x, gw, uw, dw):
            return jax.nn.silu(x @ gw.T) * (x @ uw.T) @ dw.T
        key = jax.random.key(seed)
        ks = jax.random.split(key, 9)
        std = 0.02
        return {'hidden_states': jax.random.normal(ks[0], (B, S, H), jnp.float32), 'gate_weight': jax.random.normal(ks[1], (N_EXPERTS, H), jnp.float32) * std, 'e_score_correction_bias': jnp.zeros((N_EXPERTS,), jnp.float32), 'gate_w': jax.random.normal(ks[2], (N_EXPERTS, F_MOE, H), jnp.float32) * std, 'up_w': jax.random.normal(ks[3], (N_EXPERTS, F_MOE, H), jnp.float32) * std, 'down_w': jax.random.normal(ks[4], (N_EXPERTS, H, F_MOE), jnp.float32) * std, 'sh_gate_w': jax.random.normal(ks[5], (F_SHARED, H), jnp.float32) * std, 'sh_up_w': jax.random.normal(ks[6], (F_SHARED, H), jnp.float32) * std, 'sh_down_w': jax.random.normal(ks[7], (H, F_SHARED), jnp.float32) * std}
    _L0_ffn_in = _L0_ffn_setup()
    _L0_c = _w((lambda *s: np.random.randn(*s).astype(np.float32) * 0.05)(1, 256))
    _L0_wmod = _w((lambda *s: np.random.randn(*s).astype(np.float32) * 0.05)(256, 6 * 256) * 256 ** (-0.5))
    _d = {'L0_attn_x': _L0_attn_in['x'], 'L0_attn_rms_w': _L0_attn_in['rms_w'], 'L0_attn_wq': _L0_attn_in['wq'], 'L0_attn_wk': _L0_attn_in['wk'], 'L0_attn_wv': _L0_attn_in['wv'], 'L0_attn_wo': _L0_attn_in['wo'], 'L0_ffn_gate_weight': _L0_ffn_in['gate_weight'], 'L0_ffn_e_score_correction_bias': _L0_ffn_in['e_score_correction_bias'], 'L0_ffn_gate_w': _L0_ffn_in['gate_w'], 'L0_ffn_up_w': _L0_ffn_in['up_w'], 'L0_ffn_down_w': _L0_ffn_in['down_w'], 'L0_ffn_sh_gate_w': _L0_ffn_in['sh_gate_w'], 'L0_ffn_sh_up_w': _L0_ffn_in['sh_up_w'], 'L0_ffn_sh_down_w': _L0_ffn_in['sh_down_w'], 'L0_c': _L0_c, 'L0_wmod': _L0_wmod}
    _x0 = _d['L0_attn_x']
    _d['L0_attn_x'] = jax.random.normal(jax.random.fold_in(jax.random.key(seed), 1), (1, 2048, 256), dtype=_x0.dtype)
    del _x0
    return _d

def reference(L0_attn_x, L0_attn_rms_w, L0_attn_wq, L0_attn_wk, L0_attn_wv, L0_attn_wo, L0_ffn_gate_weight, L0_ffn_e_score_correction_bias, L0_ffn_gate_w, L0_ffn_up_w, L0_ffn_down_w, L0_ffn_sh_gate_w, L0_ffn_sh_up_w, L0_ffn_sh_down_w, L0_c, L0_wmod):

    def _L0_attn_ref(x, rms_w, wq, wk, wv, wo):
        import jax, jax.numpy as jnp
        import numpy as np
        RMS_EPS = 1e-06
        ROPE_BASE = 10000.0
        WINDOW = 64
        N_HEADS = 16
        N_KV_HEADS = 4

        def _rope_cos_sin(seq_len, head_dim, dtype):
            inv_freq = 1.0 / ROPE_BASE ** (jnp.arange(0, head_dim, 2, dtype=jnp.float32) / head_dim)
            ang = jnp.arange(seq_len, dtype=jnp.float32)[:, None] * inv_freq[None, :]
            return (jnp.cos(ang).astype(dtype), jnp.sin(ang).astype(dtype))

        def _apply_rope(x, cos, sin):
            B, S, H, hd = x.shape
            xr = x.reshape(B, S, H, hd // 2, 2)
            x1, x2 = (xr[..., 0], xr[..., 1])
            c = cos[None, :, None, :]
            s = sin[None, :, None, :]
            o1 = x1 * c - x2 * s
            o2 = x1 * s + x2 * c
            return jnp.stack([o1, o2], axis=-1).reshape(B, S, H, hd)
        B, S, D = x.shape
        hd = D // N_HEADS
        n_rep = N_HEADS // N_KV_HEADS
        var = jnp.mean(jnp.square(x), axis=-1, keepdims=True)
        xn = x * jax.lax.rsqrt(var + RMS_EPS) * rms_w
        xq = (xn @ wq).reshape(B, S, N_HEADS, hd)
        xk = (xn @ wk).reshape(B, S, N_KV_HEADS, hd)
        xv = (xn @ wv).reshape(B, S, N_KV_HEADS, hd)
        cos, sin = _rope_cos_sin(S, hd, x.dtype)
        xq = _apply_rope(xq, cos, sin)
        xk = _apply_rope(xk, cos, sin)
        q = xq.transpose(0, 2, 1, 3)
        k = xk.transpose(0, 2, 1, 3)
        v = xv.transpose(0, 2, 1, 3)
        k = jnp.repeat(k, n_rep, axis=1)
        v = jnp.repeat(v, n_rep, axis=1)
        qi = jnp.arange(S)[:, None]
        ki = jnp.arange(S)[None, :]
        mask = (qi >= ki) & (qi - ki <= WINDOW)
        scale = 1.0 / np.sqrt(hd)
        scores = jnp.einsum('bhqd,bhkd->bhqk', q, k) * scale
        scores = jnp.where(mask[None, None], scores, jnp.finfo(scores.dtype).min)
        probs = jax.nn.softmax(scores, axis=-1)
        out = jnp.einsum('bhqk,bhkd->bhqd', probs, v)
        out = out.transpose(0, 2, 1, 3).reshape(B, S, D)
        return out @ wo

    def _L0_ffn_ref(hidden_states, gate_weight, e_score_correction_bias, gate_w, up_w, down_w, sh_gate_w, sh_up_w, sh_down_w):
        import jax, jax.numpy as jnp
        import numpy as np
        N_EXPERTS = 16
        TOP_K = 4
        N_GROUP = 4
        TOPK_GROUP = 2
        NORM_TOPK = True
        ROUTED_SCALE = 2.5
        H = 256
        F_MOE = 128
        F_SHARED = 256
        B, S = (2, 256)

        def _route(hidden, gate_weight, bias):
            T = hidden.shape[0]
            epg = N_EXPERTS // N_GROUP
            logits = hidden @ gate_weight.T
            scores = jax.nn.sigmoid(logits)
            scores_for_choice = scores + bias[None, :]
            grp = scores_for_choice.reshape(T, N_GROUP, epg)
            group_scores = jax.lax.top_k(grp, 2)[0].sum(-1)
            group_idx = jax.lax.top_k(group_scores, TOPK_GROUP)[1]
            group_mask = jax.nn.one_hot(group_idx, N_GROUP, dtype=jnp.bool_).any(1)
            score_mask = jnp.repeat(group_mask, epg, axis=-1)
            masked = jnp.where(score_mask, scores_for_choice, -jnp.inf)
            topk_idx = jax.lax.top_k(masked, TOP_K)[1]
            topk_weight = jnp.take_along_axis(scores, topk_idx, axis=1)
            return (topk_weight, topk_idx)

        def _swiglu(x, gw, uw, dw):
            return jax.nn.silu(x @ gw.T) * (x @ uw.T) @ dw.T
        Bh, Sh, Hh = hidden_states.shape
        hidden = hidden_states.reshape(-1, Hh)
        topk_weight, topk_idx = _route(hidden, gate_weight, e_score_correction_bias)
        if NORM_TOPK:
            topk_weight = topk_weight / (topk_weight.sum(-1, keepdims=True) + 1e-20)
        topk_weight = topk_weight * ROUTED_SCALE
        one_hot = jax.nn.one_hot(topk_idx, N_EXPERTS, dtype=topk_weight.dtype)
        weight_matrix = (one_hot * topk_weight[..., None]).sum(1)
        g = jnp.einsum('th,nfh->ntf', hidden, gate_w)
        u = jnp.einsum('th,nfh->ntf', hidden, up_w)
        act = jax.nn.silu(g) * u
        routed = jnp.einsum('ntf,nhf,tn->th', act, down_w, weight_matrix)
        out = routed + _swiglu(hidden, sh_gate_w, sh_up_w, sh_down_w)
        return out.reshape(Bh, Sh, Hh)
    x = L0_attn_x
    mod = (_silu(L0_c) @ L0_wmod).reshape(L0_c.shape[0], 6, 1, -1)
    sa, ca, ga, sb, cb, gb = (mod[:, 0], mod[:, 1], mod[:, 2], mod[:, 3], mod[:, 4], mod[:, 5])
    ga = (2 * (ga >= 0) - 1) * jnp.maximum(jnp.abs(ga), 0.25)
    gb = (2 * (gb >= 0) - 1) * jnp.maximum(jnp.abs(gb), 0.25)
    h = _layernorm(x, axis=-1) * (1 + ca) + sa
    x = x + ga * _L0_attn_ref(h, L0_attn_rms_w, L0_attn_wq, L0_attn_wk, L0_attn_wv, L0_attn_wo)
    h = _layernorm(x, axis=-1) * (1 + cb) + sb
    x = x + gb * _L0_ffn_ref(h, L0_ffn_gate_weight, L0_ffn_e_score_correction_bias, L0_ffn_gate_w, L0_ffn_up_w, L0_ffn_down_w, L0_ffn_sh_gate_w, L0_ffn_sh_up_w, L0_ffn_sh_down_w)
    return x

_drawn_inputs = setup_inputs


def setup_inputs(seed=0):
    import zlib

    import numpy as np

    out = dict(_drawn_inputs(seed))
    spreads = {'L0_attn_rms_w': (1.0, 0.6), 'L0_ffn_e_score_correction_bias': (0.0, 0.8)}
    factors = {'L0_ffn_gate_weight': 8.0,
     'L0_ffn_gate_w': 8.0,
     'L0_ffn_up_w': 8.0,
     'L0_ffn_down_w': 8.0,
     'L0_ffn_sh_gate_w': 8.0,
     'L0_ffn_sh_up_w': 8.0,
     'L0_ffn_sh_down_w': 8.0}
    for name, (base, spread) in spreads.items():
        noise = np.random.default_rng([zlib.crc32(name.encode()), seed]).standard_normal(out[name].shape)
        drawn = base * np.exp(spread * noise) if base else spread * noise
        out[name] = jnp.asarray(drawn.astype(out[name].dtype))
    for name, factor in factors.items():
        out[name] = (out[name] * factor).astype(out[name].dtype)
    return out
```

```python
from contextlib import ExitStack

import concourse.bass as bass
from concourse import mybir

F32 = mybir.dt.float32
F32R = mybir.dt.float32r
BF16 = mybir.dt.bfloat16
ALU = mybir.AluOpType
ACT = mybir.ActivationFunctionType
AX = mybir.AxisListType

P = 128
S = 2048
D = 256
KD = D // P
NH, NKV, HD = 16, 4, 16
WINDOW = 64
NQK = NH + NKV
QKV = (NH + 2 * NKV) * HD
NT = S // P
KEYS = P + WINDOW
BLK = 64
NPAIR = NH // 2
SLOT = 64
NE, TOPK, NGRP, TOPG, EPG = 16, 4, 4, 2, 4
ROUTED_SCALE = 2.5
F = 128
NF = NE + 2
CH = 512
NC = S // CH
TPC = CH // P
GU = KD * 2 * F
WCOLS = NF * GU + NF * D
WCH = WCOLS // NT
DOWN0 = NF * GU
NEG = -3.0e38
SCALE = HD ** -0.5
LN_EPS, RMS_EPS = 1e-5, 1e-6

C_ID, C_COS, C_SIN, C_TRI, C_NHALF = 0, P, P + NT * HD, P + 2 * NT * HD, P + 2 * NT * HD + 16
NCF = C_NHALF + 1
B_ID, B_MQ, B_MQ0, B_MT, B_MT0, B_SEL = 0, P, P + KEYS, P + 2 * KEYS, P + 2 * KEYS + BLK, P + 2 * KEYS + 2 * BLK
NCB = B_SEL + NE

BK_T, BK_PROJ, BK_S, BK_PV, BK_RING = 0, 1, 2, 3, 4
T_USE = [8, 9, 11, 13]
TR_USE = [10, 12, 14]


class Tile:

    def __init__(self, m, d):
        self.m, self.d, self.par = m, d, d % 2

    def __add__(self, k):
        return Tile(self.m, self.d + k)

    def times(self, per, extra=0):
        return self.m * (2 * per) + (per * self.d + extra)

    def half(self, per, extra=0):
        return self.m * per + (per * (self.d // 2) + extra)

    def static(self):
        return isinstance(self.m, int)

    def index(self):
        return self.times(1)


def bc(ap, at, n):
    dims = [list(x) for x in ap.ap]
    dims.insert(at, [0, n])
    return bass.AP(ap.tensor, ap.offset, dims)


def build(nc, x, wqkv, wo, rms_w, gate_weight, bias, wbig, c, wmod, cf, cb, out):
    x1_dram = nc.dram_tensor("x1_scratch", (S, D), F32, kind="Internal").ap()
    with ExitStack() as ctx:
        def sb(name, shape, dt=F32):
            return ctx.enter_context(nc.sbuf_tensor(name, shape, dt))

        def sem(name):
            return ctx.enter_context(nc.semaphore(name))

        banks = [ctx.enter_context(nc.psum_tensor(f"bank{i}", [P, 512], F32)) for i in range(8)]

        w_hi = sb("w_hi", [P, WCOLS], F32R)
        w_lo = sb("w_lo", [P, WCOLS], F32R)
        w_stage = sb("w_stage", [P, WCH])
        wqkv_s = sb("wqkv_s", [P, KD, QKV])
        wo_s = sb("wo_s", [P, KD, D])
        gw_s = sb("gw_s", [P, KD, NE])
        bias_s = sb("bias_s", [P, NE])
        rms_s = sb("rms_s", [P, KD])
        cf_s = sb("cf_s", [P, NCF])
        cb_s = sb("cb_s", [P, NCB], BF16)
        mod_rows = sb("mod_rows", [P, 2, D])
        mod_cols = sb("mod_cols", [P, 6])
        silu_c = sb("silu_c", [P, 4, KD])
        c_wide = sb("c_wide", [P, KD, P])
        h2_hi = sb("h2_hi", [P, KD, S], F32R)
        h2_lo = sb("h2_lo", [P, KD, S], F32R)
        xs = sb("xs", [P, 4, D])
        x1_o = sb("x1_o", [P, 2, D])
        scratch = sb("scratch", [P, 3072])
        qt = sb("qt", [P, 2, NPAIR, P], F32R)
        kt = sb("kt", [P, 2, NKV, KEYS], F32R)
        qs = sb("qs", [P, NH, SLOT])
        ks = sb("ks", [P, 2 * NKV, SLOT])
        xv = sb("xv", [P, 2 * KD * KEYS + 4 * NKV * (HD + 1)])
        xnt = xv[:, 0:2 * KD * KEYS].rearrange("p (s k t) -> p s k t", s=2, k=KD)
        vv = xv[:, 2 * KD * KEYS:].rearrange("p (s w g d) -> p s w g d", s=2, w=2, g=NKV)
        rt = sb("rt", [P, 7, D])
        logits = sb("logits", [P, NT, NE])
        wt = xv[:, 0:S // 2].bitcast(BF16)
        stat = sb("stat", [P, 2, 6])
        mv = sb("mv", [P, 2, 2])
        tiny = sb("tiny", [P, 8])
        mx = sb("mx", [P, 2, NPAIR])
        ms = sb("ms", [P, 2, 2, NPAIR])
        cb_stage = rt[:, 0:3, :].rearrange("p a b -> p (a b)")[:, 0:NCB]
        rden = sb("rden", [P, NH])
        gtmp = w_stage[:, 0:NT * 28]

        ident = cf_s[:, C_ID:C_ID + P]
        identb = cb_s[:, B_ID:B_ID + P]
        pt = [scratch[:, 512 * i:512 * i + 512] for i in range(2)]
        rope_a = scratch[:, 1024:1344]
        rope_b = scratch[:, 1344:1664]
        rope_o = scratch[:, 1664:1984]
        mt = sb("mt", [4 * NPAIR, P], F32R)
        z, h, xn, attn, attnt, z2, h32 = (rt[:, i, :] for i in range(7))
        xa = [xs[:, 0, :], xs[:, 1, :]]
        xb = [xs[:, 2, :], xs[:, 3, :]]
        ve, rstd, ssq, msq, rrms, ve2, rstd2 = (tiny[:, i:i + 1] for i in range(7))
        nhalf = cf_s[:, C_NHALF:C_NHALF + 1]
        wmod_s = scratch[:, :].rearrange("p (k n) -> p k n", k=KD)

        s_const = sem("consts_loaded")
        s_wmod = sem("wmod_loaded")
        s_small = sem("small_weights_loaded")
        s_su = sem("setup_step")
        s_su_act = sem("setup_exp")
        s_modp = sem("mod_product")
        s_ones = sem("fixed_parts_written")
        s_xa = [sem("xa_loaded0"), sem("xa_loaded1")]
        s_xb = [sem("xb_loaded0"), sem("xb_loaded1")]
        s_st = sem("ln1_stats")
        s_ag = sem("ln1_aggregated")
        s_ve = sem("ln1_variance")
        s_rstd = sem("ln1_rstd")
        s_z = sem("ln1_normal")
        s_hm = sem("h_scaled")
        s_h = sem("h_ready")
        s_ssq = sem("h_squares")
        s_msq = sem("h_mean_square")
        s_rrms = sem("h_rrms")
        s_xn = sem("xn_ready")
        s_xtr = sem("xn_transposed")
        s_xnt = sem("xnt_ready")
        s_proj = sem("projected")
        s_v = sem("v_ready")
        s_ra = sem("rope_products")
        s_ro = sem("rope_done")
        s_qkhi = sem("qk_high")
        s_qklo = sem("qk_low")
        s_qktr = sem("qk_transposed")
        s_qkt = sem("qkt_ready")
        s_sc = sem("scores_for_max")
        s_mxr = sem("max_read")
        s_ms = sem("max_parts")
        s_mtr = sem("max_transposed")
        s_mt = sem("max_rows_ready")
        s_md = sem("max_rows_placed")
        s_ts = sem("scores_transposed")
        s_ex = sem("probs_ready")
        s_pv = sem("weighted_values")
        s_rd = sem("denominator_inverted")
        s_at = sem("attn_ready")
        s_atr = sem("attn_transposed")
        s_att = sem("attnt_ready")
        s_wo = sem("attn_projected")
        s_x1 = sem("x1_ready")
        s_x1s = [sem("x1_stored0"), sem("x1_stored1")]
        s_st2 = sem("ln2_stats")
        s_ag2 = sem("ln2_aggregated")
        s_ve2 = sem("ln2_variance")
        s_rstd2 = sem("ln2_rstd")
        s_z2 = sem("z2_ready")
        s_z2tr = sem("z2_transposed")
        s_h32 = sem("h2_ready")
        s_h2hi = sem("h2_high")
        s_h2lo = sem("h2_low")
        s_lg = sem("logits_product")
        s_lgr = sem("logits_read")
        s_wl = sem("w_chunk_loaded")
        s_whi = sem("w_chunk_high")
        s_wlo = sem("w_chunk_low")

        s_r = sem("routing_step")
        s_rexp = sem("routing_exp")
        s_wtr = sem("weights_transposed")
        s_wt = sem("weights_row_ready")
        s_g = sem("gate_product")
        s_u = sem("up_product")
        s_wb = sem("expert_weight_spread")
        s_sl = sem("silu_ready")
        s_wsl = sem("weighted_silu_ready")
        s_a = sem("act_ready")
        s_ahi = sem("act_high")
        s_alo = sem("act_low")
        s_afree = sem("act_slot_free")
        s_yt = sem("ffn_scaled")
        s_ytr = sem("ffn_transposed")
        s_fin = sem("out_ready")
        s_x1l = sem("x1_chunk_loaded")
        s_out = [sem("out_stored0"), sem("out_stored1")]

        routing_steps = []
        w_parts = qs[:, 0:12, :].rearrange("p a b -> p (a b)").bitcast(BF16)[:, 0:NT * 48].rearrange("p (t q e) -> p t q e", q=3, e=NE)

        BK_G, BK_U, BK_Y, BK_WB, BK_YT = 0, 2, 4, 6, 6
        sl = [scratch[:, 0:512], scratch[:, 512:1024]]
        aa = [scratch[:, 1024:1536], scratch[:, 1536:2048]]
        wsl = scratch[:, 2048:2560]
        a_hi = [qt[:, 0, 4 * i:4 * i + 4, :].rearrange("p a b -> p (a b)") for i in range(2)]
        a_lo = [qt[:, 1, 4 * i:4 * i + 4, :].rearrange("p a b -> p (a b)") for i in range(2)]
        yt = qs[:].rearrange("p a b -> p (a b)").rearrange("p (k t) -> p k t", k=KD)

        def ytok(pr):
            return x1_o[:, :, :] if pr == 0 else vtok

        vtok = scratch[:, 2560:3072].rearrange("p (t d) -> p t d", t=2)

        sq_junk = scratch[:, 2048:2304]
        ks2 = bass.AP(ks[:].tensor, ks[:].offset, [list(ks[:].ap[0]), [2 * SLOT, NKV], [2 * HD, 4], [1, HD]]).bitcast(F32R)
        k4 = ks[:].rearrange("p (g r) d -> p g r d", r=2)
        SETUP_STEPS = 19

        block = ctx.enter_context(nc.Block())

        LAST = 4

        def turns(eng, body):
            for j in range(LAST):
                body(Tile(0, j), j)
            with eng.Fori(LAST // 2, NT // 2) as m:
                for k in range(2):
                    body(Tile(m, k), None)
            for j in range(NT, NT + LAST):
                body(Tile(0, j), j)

        def live(j, lag):
            return j is None or 0 <= j - lag < NT

        def after(j, lag, back=1):
            return j is None or j - lag - back >= 0

        def ring(u):
            return banks[BK_RING + u % 4]

        @block.sync
        def _(sp):
            sp.dma_start(cf_s[:], cf).then_inc(s_const, 16)
            sp.dma_start(cb_stage, cb).then_inc(s_const, 16)
            sp.dma_start(silu_c[:, 0, :], c).then_inc(s_const, 16)
            sp.dma_start(xa[0], x[0:P, :]).then_inc(s_xa[0], 16)
            for k in range(KD):
                sp.dma_start(wmod_s[:, k, :], wmod[P * k:P * (k + 1), :]).then_inc(s_wmod, 16)
            sp.dma_start(wqkv_s[:], wqkv.rearrange("(k p) n -> p k n", p=P)).then_inc(s_small, 16)
            sp.dma_start(wo_s[:], wo.rearrange("(k p) n -> p k n", p=P)).then_inc(s_small, 16)
            sp.dma_start(gw_s[:], gate_weight.rearrange("(k p) n -> p k n", p=P)).then_inc(s_small, 16)
            sp.dma_start(rms_s[:], rms_w).then_inc(s_small, 16)
            sp.dma_start(bias_s[:], bc(bias.rearrange("(o n) -> o n", o=1)[0, :], 0, P)).then_inc(s_small, 16)

            def body(t, j):
                if live(j, 0) and j != 0:
                    if after(j, 0, 2):
                        sp.wait_ge(s_z, t.times(1, -1))
                    sp.dma_start(xa[t.par], x[bass.ds(t.times(P), P), :]).then_inc(s_xa[t.par], 16)
                if live(j, 0):
                    if after(j, 0):
                        sp.wait_ge(s_wlo, t.times(1))
                    sp.dma_start(w_stage[:], wbig[bass.ds(t.index(), 1), :, :].rearrange("o p n -> (o p) n")).then_inc(s_wl, 16)
                n = t + (-2)
                if live(j, 2):
                    if after(j, 2, 2):
                        sp.wait_ge(s_x1, n.times(1, -1))
                    sp.dma_start(xb[n.par], x[bass.ds(n.times(P), P), :]).then_inc(s_xb[n.par], 16)
                    sp.wait_ge(s_mt, n.times(1, 1))
                    for hf in range(2):
                        for part in range(2):
                            r = (2 * hf + part) * NPAIR
                            row = 64 * hf + 3 * HD + part
                            sp.dma_start(qt[row:row + 1, n.par, :, :].bitcast(F32), mt[r:r + NPAIR, :].bitcast(F32)).then_inc(s_md, 16)
                n = t + (-3)
                if live(j, 3):
                    sp.wait_ge(s_x1, n.times(1, 1))
                    sp.dma_start(x1_dram[bass.ds(n.times(P), P), :], x1_o[:, n.par, :]).then_inc(s_x1s[n.par], 16)

            turns(sp, body)
            for par in range(2):
                sp.wait_ge(s_x1s[par], 16 * NT // 2)
            for pr in range(2):
                sp.sem_inc(s_out[pr], 16)
            with sp.Fori(0, NC) as ci:
                sp.wait_ge(s_fin, ci * 2 + 2)
                sp.dma_start(xs[:], x1_dram[bass.ds(ci * CH, CH), :].rearrange("(t p) d -> p t d", p=P)).then_inc(s_x1l, 16)
                for pr in range(2):
                    sp.wait_ge(s_fin, ci * 2 + (pr + 3))
                    sp.dma_start(out[bass.ds(ci * CH + 2 * P * pr, 2 * P), :].rearrange("(t p) d -> p t d", p=P),
                                 ytok(pr)).then_inc(s_out[pr], 16)
            for pr in range(2):
                sp.wait_ge(s_out[pr], 16 * NC + 16)

        @block.gpsimd
        def _(pool):
            g = nc.gpsimd
            pool.wait_ge(s_const, 48)

            def body(t, j):
                if live(j, 0):
                    pool.wait_ge(s_ve, t.times(1, 1))
                    g.tensor_tensor(rstd, ve, nhalf, ALU.pow).then_inc(s_rstd, 1)
                n = t + (-3)
                if live(j, 0):
                    pool.wait_ge(s_z, t.times(1, 1))
                    if j == 0:
                        pool.wait_ge(s_su, SETUP_STEPS)
                    if after(j, 0):
                        pool.wait_ge(s_xn, t.times(1))
                    g.tensor_tensor(h, z, mod_rows[:, 1, :], ALU.mult).then_inc(s_hm, 1)
                    pool.wait_ge(s_hm, t.times(1, 1))
                    g.tensor_tensor(h, h, mod_rows[:, 0, :], ALU.add).then_inc(s_h, 1)
                if live(j, 3):
                    pool.wait_ge(s_ve2, n.times(1, 1))
                    g.tensor_tensor(rstd2, ve2, nhalf, ALU.pow).then_inc(s_rstd2, 1)
                n = t + (-1)
                if live(j, 1):
                    pool.wait_ge(s_qkhi, n.times(2, 2))
                    o = rope_o.rearrange("p (n d) -> p n d", d=HD)
                    if after(j, 1):
                        pool.wait_ge(s_qktr, n.times(3))
                    g.tensor_tensor(qs[:, :, 2 * HD:3 * HD].bitcast(F32R), o[:, 0:NH, :], qs[:, :, 0:HD], ALU.subtract).then_inc(s_qklo, 1)
                    g.tensor_tensor(k4[:, :, :, HD:2 * HD].bitcast(F32R), bc(o[:, NH:NQK, :], 2, 2), k4[:, :, :, 0:HD], ALU.subtract).then_inc(s_qklo, 1)
                if live(j, 0):
                    pool.wait_ge(s_msq, t.times(1, 1))
                    g.tensor_tensor(rrms, msq, nhalf, ALU.pow).then_inc(s_rrms, 1)
                    pool.wait_ge(s_whi, t.times(1, 1))
                    pool.wait_ge(s_const, 48)
                    at = t.times(WCH)
                    g.tensor_tensor(w_lo[:, bass.ds(at, WCH)], w_stage[:], w_hi[:, bass.ds(at, WCH)].bitcast(F32), ALU.subtract).then_inc(s_wlo, 1)

            turns(pool, body)

        @block.vector
        def _(dve):
            v = nc.vector
            step = [0]

            def chain(ins, sem_=s_su):
                step[0] += 1
                ins.then_inc(sem_, 1)
                dve.wait_ge(sem_, step[0])

            v.memset(qs[:], 0.0).then_inc(s_ones, 1)
            v.memset(ks[:], 0.0).then_inc(s_ones, 1)
            v.memset(kt[:, 0, :, 0:WINDOW].bitcast(F32), 0.0).then_inc(s_ones, 1)
            v.memset(xnt[:, 0, :, 0:WINDOW], 0.0).then_inc(s_ones, 1)
            v.memset(vv, 1.0).then_inc(s_ones, 1)
            dve.wait_ge(s_ones, 5)
            v.memset(ks[:, :, 3 * HD:3 * HD + 2], -1.0).then_inc(s_ones, 1)

            dve.wait_ge(s_const, 48)
            v.tensor_copy(cb_s[:], cb_stage).then_inc(s_ones, 1)
            dve.wait_ge(s_su_act, 1)
            chain(v.tensor_scalar(silu_c[:, 2, :], silu_c[:, 1, :], 1.0, None, ALU.add))
            chain(v.reciprocal(silu_c[:, 3, :], silu_c[:, 2, :]))
            chain(v.tensor_tensor(silu_c[:, 1, :], silu_c[:, 0, :], silu_c[:, 3, :], ALU.mult))
            chain(v.tensor_copy(c_wide[:], bc(silu_c[:, 1, :], 2, P)))
            dve.wait_ge(s_modp, 1)
            chain(v.tensor_copy(mod_rows[:, 0, :], banks[4][:, 0:D]))
            chain(v.tensor_scalar(mod_rows[:, 1, :], banks[4][:, D:2 * D], 1.0, None, ALU.add))
            chain(v.tensor_copy(mod_cols[:], banks[6][:, 0:6]))
            chain(v.tensor_scalar(mod_cols[:, 2:4], mod_cols[:, 2:4], 1.0, None, ALU.add))

            def gate(g, mag, sgn, to):
                chain(v.tensor_copy(sgn, g))
                chain(v.scalar_tensor_tensor(mag, sgn, -1.0, sgn, ALU.mult, ALU.max))
                chain(v.tensor_scalar(mag, mag, 0.25, None, ALU.max))
                chain(v.tensor_scalar(sgn, g, 0.0, 2.0, ALU.is_ge, ALU.mult))
                return v.scalar_tensor_tensor(to, sgn, -1.0, mag, ALU.add, ALU.mult)

            chain(gate(banks[5][:, 0:D], attn, attnt, z2))
            chain(gate(mod_cols[:, 4:6], tiny[:, 0:2], tiny[:, 2:4], mod_cols[:, 4:6]))
            dve.wait_ge(s_small, 80)
            chain(v.tensor_tensor(wo_s[:], wo_s[:], bc(z2, 1, KD), ALU.mult))
            for k in range(KD):
                ins = v.tensor_scalar(wqkv_s[:, k, :], wqkv_s[:, k, :], rms_s[:, k:k + 1], None, ALU.mult)
                ins.then_inc(s_ones, 1)
            assert step[0] == SETUP_STEPS, step[0]

            def norm1(t, j):
                dve.wait_ge(s_xa[t.par], t.half(16, 16))
                v.bn_stats(stat[:, 0, :], xa[t.par]).then_inc(s_st, 1)
                dve.wait_ge(s_st, t.times(1, 1))
                v.tensor_copy(tiny[:, 7:8], stat[:, 0, 0:1])
                v.bn_aggr(mv[:, 0, :], stat[:, 0, :]).then_inc(s_ag, 1)
                dve.wait_ge(s_ag, t.times(1, 1))
                v.tensor_scalar(ve, mv[:, 0, 1:2], LN_EPS, None, ALU.add).then_inc(s_ve, 1)

            def maxima(t, uses):
                for u in uses:
                    a, hf = u // 2, u % 2
                    dve.wait_ge(s_sc, t.times(8, u + 1))
                    v.tensor_reduce(mx[:, hf, 2 * a:2 * a + 2],
                                    ring(u)[:, 0:2 * KEYS].rearrange("p (h k) -> p h k", h=2),
                                    AX.X, ALU.max).then_inc(s_mxr, 1)

            def body(t, j):
                n = t + (-3)
                if live(j, 3):
                    pv = banks[BK_PV][:, 0:NH * (HD + 1)].rearrange("p (h d) -> p h d", h=NH)
                    dve.wait_ge(s_pv, n.times(4, 4))
                    v.reciprocal(rden[:], pv[:, :, HD]).then_inc(s_rd, 1)
                    dve.wait_ge(s_rd, n.times(1, 1))
                    if after(j, 3):
                        dve.wait_ge(s_atr, n.times(1))
                    v.tensor_tensor(attn.rearrange("p (h d) -> p h d", h=NH), pv[:, :, 0:HD],
                                    bc(rden[:], 2, HD), ALU.mult).then_inc(s_at, 1)
                n = t + (-4)
                if live(j, 4):
                    dve.wait_ge(s_z2tr, n.times(1, 1))
                    if after(j, 4):
                        dve.wait_ge(s_lg, n.times(1))
                    for k in range(KD):
                        v.tensor_scalar(h32[:, P * k:P * (k + 1)], banks[BK_T][:, P * k:P * (k + 1)],
                                        mod_cols[:, 2 + k:3 + k], mod_cols[:, k:k + 1],
                                        ALU.mult, ALU.add).then_inc(s_h32, 1)
                    dve.wait_ge(s_h32, n.times(2, 2))
                    h3 = h32.rearrange("p (k t) -> p k t", k=KD)
                    at = bass.ds(n.times(P), P)
                    v.tensor_scalar(h2_hi[:, :, at], h3, 1.0, None, ALU.mult).then_inc(s_h2hi, 1)
                    dve.wait_ge(s_h2hi, n.times(1, 1))
                    v.tensor_tensor(h2_lo[:, :, at], h3, h2_hi[:, :, at].bitcast(F32), ALU.subtract).then_inc(s_h2lo, 1)
                if live(j, 0):
                    norm1(t, j)
                n = t + (-2)
                if live(j, 2):
                    if after(j, 2):
                        dve.wait_ge(s_ms, n.times(2))
                    maxima(n, range(4))
                if live(j, 0):
                    dve.wait_ge(s_rstd, t.times(1, 1))
                    if after(j, 0):
                        dve.wait_ge(s_h, t.times(1))
                    v.tensor_scalar(z, xa[t.par], mv[:, 0, 0:1], rstd, ALU.subtract, ALU.mult).then_inc(s_z, 1)
                if live(j, 2):
                    maxima(n, range(4, 8))
                    dve.wait_ge(s_mxr, n.times(8, 8))
                    if after(j, 2):
                        dve.wait_ge(s_mtr, n.times(1))
                    v.tensor_copy(ms[:, :, 0, :].bitcast(F32R), mx[:]).then_inc(s_ms, 1)
                    dve.wait_ge(s_ms, n.times(2, 1))
                    v.tensor_tensor(ms[:, :, 1, :].bitcast(F32R), mx[:], ms[:, :, 0, :], ALU.subtract).then_inc(s_ms, 1)
                n = t + (-3)
                if live(j, 3):
                    dve.wait_ge(s_wo, n.times(1, 1))
                    dve.wait_ge(s_xb[n.par], n.half(16, 16))
                    if after(j, 3, 2):
                        dve.wait_ge(s_x1s[n.par], n.half(16))
                    v.tensor_tensor(x1_o[:, n.par, :], banks[BK_PV][:, 0:D], xb[n.par], ALU.add).then_inc(s_x1, 1)
                    dve.wait_ge(s_x1, n.times(1, 1))
                    v.bn_stats(stat[:, 1, :], x1_o[:, n.par, :]).then_inc(s_st2, 1)
                    dve.wait_ge(s_st2, n.times(1, 1))
                    v.tensor_copy(tiny[:, 7:8], stat[:, 1, 0:1])
                    v.bn_aggr(mv[:, 1, :], stat[:, 1, :]).then_inc(s_ag2, 1)
                    dve.wait_ge(s_ag2, n.times(1, 1))
                    v.tensor_scalar(ve2, mv[:, 1, 1:2], LN_EPS, None, ALU.add).then_inc(s_ve2, 1)
                n = t + (-1)
                if live(j, 1):
                    dve.wait_ge(s_proj, n.times(1, 1))
                    src = banks[BK_PROJ][:, 0:NQK * HD].rearrange("p (n d) -> p n d", d=HD)
                    sw = bass.AP(src.tensor, src.offset + 1, [list(src.ap[0]), [HD, NQK], [2, HD // 2], [-1, 2]])
                    cos = bc(cf_s[:, bass.ds(n.times(HD, C_COS), HD)], 1, NQK)
                    sin = bc(cf_s[:, bass.ds(n.times(HD, C_SIN), HD)].rearrange("p (i j) -> p i j", j=2), 1, NQK)
                    v.tensor_tensor(rope_a.rearrange("p (n d) -> p n d", d=HD), src, cos, ALU.mult).then_inc(s_ra, 1)
                    v.tensor_tensor(rope_b.rearrange("p (n i j) -> p n i j", i=HD // 2, j=2), sw, sin, ALU.mult).then_inc(s_ra, 1)
                    dve.wait_ge(s_ra, n.times(2, 2))
                    if after(j, 1):
                        dve.wait_ge(s_qklo, n.times(2))
                    v.tensor_tensor(rope_o, rope_a, rope_b, ALU.add).then_inc(s_ro, 1)
                n = t + (-4)
                if live(j, 4):
                    dve.wait_ge(s_lg, n.times(1, 1))
                    v.tensor_scalar(logits[:, bass.ds(n.index(), 1), :].rearrange("p o e -> p (o e)"),
                                    banks[BK_S][:, 0:NE], 1.0, None, ALU.mult).then_inc(s_lgr, 1)
                if live(j, 0):
                    dve.wait_ge(s_ssq, t.times(1, 1))
                    v.tensor_scalar(msq, ssq, 1.0 / D, RMS_EPS, ALU.mult, ALU.add).then_inc(s_msq, 1)
                n = t + (-3)
                if live(j, 3):
                    dve.wait_ge(s_rstd2, n.times(1, 1))
                    if after(j, 3):
                        dve.wait_ge(s_z2tr, n.times(1))
                    v.tensor_scalar(z2, x1_o[:, n.par, :], mv[:, 1, 0:1], rstd2, ALU.subtract, ALU.mult).then_inc(s_z2, 1)
                if live(j, 0):
                    dve.wait_ge(s_rrms, t.times(1, 1))
                    if after(j, 0):
                        dve.wait_ge(s_xtr, t.times(1))
                    v.tensor_scalar(xn, h, rrms, None, ALU.mult).then_inc(s_xn, 1)

            turns(dve, body)

            E3 = lambda a: a.rearrange("p (t e) -> p t e", e=NE)
            G4 = lambda a: a.rearrange("p (t g e) -> p t g e", g=NGRP, e=EPG)
            ex, sc, ch, mk, rep, wgt, tmp = (rt[:, i, :] for i in range(7))
            step[0] = 0

            def link(ins):
                chain(ins, s_r)

            dve.wait_ge(s_rexp, 1)
            dve.wait_ge(s_wlo, NT)
            link(v.tensor_scalar(tmp, ex, 1.0, None, ALU.add))
            link(v.reciprocal(sc, tmp))
            link(v.tensor_tensor(E3(ch), E3(sc), bc(bias_s[:], 1, NT), ALU.add))
            c4 = G4(ch)
            prs = gtmp[:, 0:NT * 24].rearrange("p (t g s) -> p t g s", g=NGRP, s=6)
            v.tensor_tensor(prs[:, :, :, 0:3], c4[:, :, :, 0:3], c4[:, :, :, 1:4], ALU.add)
            v.tensor_tensor(prs[:, :, :, 3:5], c4[:, :, :, 0:2], c4[:, :, :, 2:4], ALU.add)
            link(v.tensor_tensor(prs[:, :, :, 5:6], c4[:, :, :, 0:1], c4[:, :, :, 3:4], ALU.add))
            gs = gtmp[:, NT * 24:NT * 28].rearrange("p (t g) -> p t g", g=NGRP)
            link(v.tensor_reduce(gs, prs, AX.X, ALU.max))
            other, own = bc(gs, 2, NGRP), bc(gs, 3, NGRP)
            tri = bc(cf_s[:, C_TRI:C_TRI + 16].rearrange("p (a b) -> p a b", b=NGRP), 1, NT)
            v.tensor_tensor(G4(tmp), other, own, ALU.is_gt)
            link(v.tensor_tensor(G4(ex), other, own, ALU.is_equal))
            link(v.tensor_tensor(G4(ex), G4(ex), tri, ALU.mult))
            link(v.tensor_tensor(tmp, tmp, ex, ALU.add))
            rank = gtmp[:, 0:NT * NGRP].rearrange("p (t g) -> p t g", g=NGRP)
            link(v.tensor_reduce(rank, G4(tmp), AX.X, ALU.add))
            gm = gtmp[:, NT * NGRP:2 * NT * NGRP].rearrange("p (t g) -> p t g", g=NGRP)
            gn = gtmp[:, 2 * NT * NGRP:3 * NT * NGRP].rearrange("p (t g) -> p t g", g=NGRP)
            v.tensor_scalar(gm, rank, TOPG - 0.5, None, ALU.is_lt)
            link(v.tensor_scalar(gn, rank, TOPG - 0.5, NEG, ALU.is_gt, ALU.mult))
            link(v.tensor_tensor(G4(mk), G4(ch), bc(gm, 3, EPG), ALU.mult))
            link(v.tensor_tensor(G4(mk), G4(mk), bc(gn, 3, EPG), ALU.add))
            top = gtmp[:, 0:NT * 8].rearrange("p (t k) -> p t k", k=8)
            for i in range(NT):
                ins = v.max(top[:, i, :], E3(mk)[:, i, :])
            link(ins)
            link(v.memset(top[:, :, TOPK:8], 2.0e38))
            for i in range(NT):
                ins = v.match_replace(E3(rep)[:, i, :], top[:, i, :], E3(mk)[:, i, :], -NEG)
            link(ins)
            link(v.tensor_scalar(rep, rep, 1.0e38, None, ALU.is_gt))
            link(v.tensor_tensor(wgt, sc, rep, ALU.mult))
            sm = gtmp[:, 0:NT]
            link(v.tensor_reduce(sm, E3(wgt), AX.X, ALU.add))
            link(v.tensor_scalar(sm, sm, 1e-20, None, ALU.add))
            link(v.reciprocal(gtmp[:, NT:2 * NT], sm))
            link(v.tensor_tensor(E3(wgt), E3(wgt), bc(gtmp[:, NT:2 * NT], 2, NE), ALU.mult))
            link(v.tensor_scalar(wgt, wgt, ROUTED_SCALE, None, ALU.mult))
            parts = w_parts
            link(v.tensor_copy(parts[:, :, 0, :], E3(wgt)))
            link(v.tensor_tensor(E3(tmp), E3(wgt), parts[:, :, 0, :], ALU.subtract))
            link(v.tensor_copy(parts[:, :, 1, :], E3(tmp)))
            link(v.tensor_tensor(parts[:, :, 2, :], E3(tmp), parts[:, :, 1, :], ALU.subtract))
            routing_steps.append(step[0])
            v.memset(xv[:, 0:S // 2], 0.0).then_inc(s_wt, 1)
            dve.wait_ge(s_wt, 1)
            for i in range(2):
                dve.wait_ge(s_wtr, i + 1)
                v.tensor_copy(wt[0:48, 1024 * i:1024 * (i + 1)], banks[7][0:48, :].bitcast(BF16)).then_inc(s_wt, 1)

            def act_(ci, i):
                nn = ci * NF + i
                dve.wait_ge(s_u, nn + 1)
                left = sl[i % 2] if i < 2 else wsl
                if i < 2:
                    dve.wait_ge(s_sl, nn + 3)
                else:
                    dve.wait_ge(s_wsl, ci * NE + i)
                v.tensor_tensor(aa[i % 2], left, banks[BK_U + i % 2][:], ALU.mult).then_inc(s_a, 1)

            def low(ci, i):
                nn = ci * NF + i
                dve.wait_ge(s_ahi, nn + 1)
                v.tensor_tensor(a_lo[i % 2], aa[i % 2], a_hi[i % 2].bitcast(F32), ALU.subtract).then_inc(s_alo, 1)

            def weighted(ci, i):
                nn = ci * NF + i
                dve.wait_ge(s_sl, nn + 3)
                dve.wait_ge(s_wb, ci * NE + (i - 1))
                v.tensor_tensor(wsl, sl[i % 2], banks[BK_WB][:], ALU.mult).then_inc(s_wsl, 1)

            dve.sem_inc(s_a, 2)
            dve.sem_inc(s_wsl, 1)
            dve.sem_inc(s_fin, 2)
            with dve.Fori(0, NC) as ci:
                for i in range(NF):
                    act_(ci, i)
                    low(ci, i)
                    if 2 <= i + 1 < NF:
                        weighted(ci, i + 1)
                for pr in range(2):
                    dve.wait_ge(s_ytr, ci * 2 + (pr + 1))
                    if pr == 0:
                        dve.wait_ge(s_x1l, ci * 16 + 16)
                    dve.wait_ge(s_out[pr], ci * 16 + 16)
                    v.tensor_tensor(ytok(pr), banks[BK_YT + pr][:].rearrange("p (t d) -> p t d", t=2),
                                    xs[:, 2 * pr:2 * pr + 2, :], ALU.add).then_inc(s_fin, 1)

        @block.scalar
        def _(act):
            a = nc.scalar
            act.wait_ge(s_const, 48)
            a.activation(silu_c[:, 1, :], silu_c[:, 0, :], ACT.Exp, scale=-1.0).then_inc(s_su_act, 1)

            def exps(n, j, i):
                u = T_USE[i]
                act.wait_ge(s_ts, n.times(4, i + 1))
                if i >= 2 or after(j, 2):
                    act.wait_ge(s_pv, n.times(4, i - 1))
                a.activation(pt[i % 2], ring(u)[:], ACT.Exp, scale=SCALE).then_inc(s_ex, 1)

            def evac(n, j, i):
                act.wait_ge(s_qktr, n.times(3, i + 1))
                b = ring(TR_USE[i])[:].rearrange("p (a t) -> p a t", t=P)
                if i == 0 and after(j, 1, 2):
                    act.wait_ge(s_ts, n.times(4, -4))
                if i < 2:
                    a.activation(qt[:, n.par, 4 * i:4 * i + 4, :], b, ACT.Copy).then_inc(s_qkt, 1)
                else:
                    if after(j, 1):
                        act.wait_ge(s_qkt, n.times(4))
                        a.activation(kt[:, n.par, :, 0:WINDOW], kt[:, 1 - n.par, :, P:KEYS].bitcast(F32), ACT.Copy).then_inc(s_qkt, 1)
                    a.activation(kt[:, n.par, :, WINDOW:KEYS], b, ACT.Copy).then_inc(s_qkt, 1 if after(j, 1) else 2)

            def body(t, j):
                n = t + (-1)
                if live(j, 1):
                    act.wait_ge(s_xtr, n.times(1, 1))
                    if after(j, 1, 2):
                        act.wait_ge(s_proj, n.times(1, -1))
                    a.activation(xnt[:, n.par, :, WINDOW:KEYS], banks[BK_T][:, 0:D].rearrange("p (k t) -> p k t", k=KD),
                                 ACT.Copy).then_inc(s_xnt, 1 if after(j, 1) else 2)
                    if after(j, 1):
                        a.activation(xnt[:, n.par, :, 0:WINDOW], xnt[:, 1 - n.par, :, P:KEYS], ACT.Copy).then_inc(s_xnt, 1)
                n = t + (-3)
                if live(j, 3):
                    act.wait_ge(s_atr, n.times(1, 1))
                    if after(j, 3):
                        act.wait_ge(s_wo, n.times(1))
                    a.activation(attnt, banks[BK_S][:, 0:D], ACT.Copy).then_inc(s_att, 1)
                if live(j, 0):
                    act.wait_ge(s_h, t.times(1, 1))
                    if after(j, 0):
                        act.wait_ge(s_msq, t.times(1))
                    a.activation(sq_junk, h, ACT.Square, accum_out=ssq).then_inc(s_ssq, 1)
                    act.wait_ge(s_wl, t.times(16, 16))
                    act.wait_ge(s_const, 48)
                    a.activation(w_hi[:, bass.ds(t.times(WCH), WCH)], w_stage[:], ACT.Copy).then_inc(s_whi, 1)
                n = t + (-2)
                if live(j, 2):
                    act.wait_ge(s_mtr, n.times(1, 1))
                    if after(j, 2):
                        act.wait_ge(s_md, n.times(64))
                    a.activation(mt[:], banks[BK_S][0:4 * NPAIR, 0:P], ACT.Copy).then_inc(s_mt, 1)
                n = t + (-1)
                if live(j, 1):
                    act.wait_ge(s_ra, n.times(2, 2))
                    if j == 1:
                        act.wait_ge(s_ones, 9)
                    if after(j, 1, 2):
                        act.wait_ge(s_pv, n.times(4, -4))
                    a.activation(vv[:, n.par, :, :, 0:HD],
                                 banks[BK_PROJ][:, NQK * HD:NQK * HD + 2 * NKV * HD].rearrange("p (w g d) -> p w g d", w=2, g=NKV),
                                 ACT.Copy).then_inc(s_v, 1)
                    act.wait_ge(s_ro, n.times(1, 1))
                    if after(j, 1):
                        act.wait_ge(s_qktr, n.times(3))
                    o = rope_o.rearrange("p (n d) -> p n d", d=HD)
                    a.activation(qs[:, :, 0:2 * HD].rearrange("p h (r d) -> p h r d", r=2).bitcast(F32R),
                                 bc(o[:, 0:NH, :], 2, 2), ACT.Copy).then_inc(s_qkhi, 1)
                    a.activation(ks2, bc(o[:, NH:NQK, :], 2, 4), ACT.Copy).then_inc(s_qkhi, 1)
                m = t + (-2)
                for i in range(4):
                    if live(j, 2):
                        exps(m, j, i)
                    if live(j, 1) and i >= 1:
                        evac(n, j, i - 1)

            turns(act, body)

            act.wait_ge(s_lgr, NT)
            a.activation(rt[:, 0, :], logits[:].rearrange("p t e -> p (t e)"), ACT.Exp, scale=-1.0).then_inc(s_rexp, 1)

            act.sem_inc(s_sl, 2)
            act.sem_inc(s_yt, 2)
            with act.Fori(0, NC) as ci:
                for i in range(NF + 1):
                    nn = ci * NF + i
                    if i >= 1:
                        act.wait_ge(s_a, nn + 2)
                        act.wait_ge(s_afree, nn)
                        a.activation(a_hi[(i - 1) % 2], aa[(i - 1) % 2], ACT.Copy).then_inc(s_ahi, 1)
                    if i < NF:
                        act.wait_ge(s_g, nn + 1)
                        act.wait_ge(s_a, nn + 1)
                        a.activation(sl[i % 2], banks[BK_G + i % 2][:], ACT.Silu).then_inc(s_sl, 1)
                for k in range(KD):
                    act.wait_ge(s_afree, ci * NF + (NF + 2))
                    a.activation(yt[:, k, :], banks[BK_Y + k][:], ACT.Copy, scale=mod_cols[:, 4 + k:5 + k]).then_inc(s_yt, 1)


        @block.tensor
        def _(pe):
            mm = nc.tensor.matmul
            tr = nc.tensor.transpose

            pe.wait_ge(s_su, 4)
            pe.wait_ge(s_wmod, 16 * KD)
            for bank, lo_, n_ in ((4, 0, 2 * D), (5, 2 * D, D)):
                for k in range(KD):
                    mm(banks[bank][:, 0:n_], c_wide[:, k, :], wmod_s[:, k, lo_:lo_ + n_], start=(k == 0), stop=(k == KD - 1))
            for i in range(6):
                for k in range(KD):
                    last = mm(banks[6][:, i:i + 1], wmod_s[:, k, 3 * D + P * i:3 * D + P * (i + 1)], silu_c[:, 1, k:k + 1],
                              start=(k == 0), stop=(k == KD - 1))
            last.then_inc(s_modp, 1)
            pe.wait_ge(s_ones, 9)
            pe.wait_ge(s_const, 48)
            pe.wait_ge(s_su, SETUP_STEPS)

            def free(n_max, n_t, n_q, j, u):
                v_ = u - 4 if u >= 4 else (u + 12 if u < 3 else 11)
                same = u >= 4
                if v_ < 8:
                    if live(j, 2):
                        pe.wait_ge(s_mxr, n_max.times(8, v_ + 1))
                    return
                if v_ in T_USE:
                    i = T_USE.index(v_)
                    if same and live(j, 2):
                        pe.wait_ge(s_ex, n_t.times(4, i + 1))
                    elif not same and (j is None or j - 3 >= 0):
                        pe.wait_ge(s_ex, n_t.times(4, i - 3))
                    return
                i = TR_USE.index(v_)
                if same and live(j, 1):
                    pe.wait_ge(s_qkt, n_q.times(4, min(i + 1, 4)))
                elif not same and (j is None or j - 2 >= 0):
                    pe.wait_ge(s_qkt, n_q.times(4, (i + 1 if i < 2 else 4) - 4))

            def maxpass(n, j, uses, first):
                for u in uses:
                    a_, hf = u // 2, u % 2
                    free(n, n, n + 1, j, u)
                    mq = B_MQ0 if first else B_MQ
                    mm(ring(u)[:, 0:2 * KEYS], identb, bc(cb_s[:, mq:mq + KEYS], 1, 2), start=True, stop=True)
                    for i in range(2):
                        p_ = 2 * a_ + i
                        last = mm(ring(u)[:, i * KEYS:(i + 1) * KEYS], qt[64 * hf:64 * hf + 3 * HD, n.par, p_, :],
                                  kt[64 * hf:64 * hf + 3 * HD, n.par, p_ // 2, :], start=False, stop=True, skip_group_check=True)
                    last.then_inc(s_sc, 1)

            def tpass(n, j, i, first):
                b2, hf = i // 2, i % 2
                u = T_USE[i]
                free(n, n, n + 1, j, u)
                mq = B_MT0 if first and b2 == 0 else B_MT
                mm(ring(u)[:], identb, bc(cb_s[:, mq:mq + BLK], 1, NPAIR), start=True, stop=True)
                R = 3 * HD + 2
                for g_ in range(NKV):
                    last = mm(ring(u)[:, P * g_:P * (g_ + 1)], kt[64 * hf:64 * hf + R, n.par, g_, BLK * b2:BLK * b2 + P],
                              qt[64 * hf:64 * hf + R, n.par, 2 * g_:2 * g_ + 2, BLK * b2:BLK * (b2 + 1)],
                              start=False, stop=True, skip_group_check=True)
                last.then_inc(s_ts, 1)

            def values(n, i):
                b2, hf = i // 2, i % 2
                pe.wait_ge(s_ex, n.times(4, i + 1))
                if i == 0:
                    pe.wait_ge(s_v, n.times(1, 1))
                for p_ in range(NPAIR):
                    h_ = 2 * p_ + hf
                    last = mm(banks[BK_PV][BLK * b2:BLK * (b2 + 1), h_ * (HD + 1):(h_ + 1) * (HD + 1)],
                              pt[i % 2][:, BLK * p_:BLK * (p_ + 1)], vv[:, n.par, 1 - b2, p_ // 2, :], start=True, stop=True)
                last.then_inc(s_pv, 1)

            def qktr(n, j, i):
                u = TR_USE[i]
                free(n + (-1), n + (-1), n, j, u)
                for a_ in range(4):
                    if i < 2:
                        p_ = 4 * i + a_
                        src = qs[:, 2 * p_:2 * p_ + 2, :].rearrange("p a b -> p (a b)")
                    else:
                        src = ks[:, 2 * a_:2 * a_ + 2, :].rearrange("p a b -> p (a b)")
                    last = tr(ring(u)[:, P * a_:P * (a_ + 1)], src, ident)
                last.then_inc(s_qktr, 1)

            def body(t, j):
                n = t + (-4)
                if live(j, 4):
                    pe.wait_ge(s_z2, n.times(1, 1))
                    pe.wait_ge(s_xnt, (t + (-1)).times(2) if live(j, 1) else 2 * NT)
                    for k in range(KD):
                        last = tr(banks[BK_T][:, P * k:P * (k + 1)], z2[:, P * k:P * (k + 1)], ident)
                    last.then_inc(s_z2tr, 1)
                n = t + (-2)
                if live(j, 2):
                    pe.wait_ge(s_qkt, n.times(4, 4))
                    maxpass(n, j, range(4), j == 2)
                n = t + (-1)
                if live(j, 1):
                    pe.wait_ge(s_xn, n.times(1, 1))
                    if live(j, 4):
                        pe.wait_ge(s_h32, (t + (-4)).times(2, 2))
                    elif after(j, 1):
                        pe.wait_ge(s_xnt, n.times(2))
                    for k in range(KD):
                        last = tr(banks[BK_T][:, P * k:P * (k + 1)], xn[:, P * k:P * (k + 1)], ident)
                    last.then_inc(s_xtr, 1)
                n = t + (-2)
                if live(j, 2):
                    maxpass(n, j, range(4, 8), j == 2)
                n = t + (-3)
                if live(j, 3):
                    pe.wait_ge(s_at, n.times(1, 1))
                    if after(j, 3, 2):
                        pe.wait_ge(s_lgr, n.times(1, -1))
                    elif after(j, 3, 0):
                        pe.wait_ge(s_mt, n.times(1, 1))
                    for k in range(KD):
                        last = tr(banks[BK_S][:, P * k:P * (k + 1)], attn[:, P * k:P * (k + 1)], ident)
                    last.then_inc(s_atr, 1)
                n = t + (-1)
                if live(j, 1):
                    pe.wait_ge(s_xnt, n.times(2, 2))
                    if after(j, 1):
                        pe.wait_ge(s_v, n.times(1))
                        pe.wait_ge(s_ra, n.times(2))
                    for k in range(KD):
                        mm(banks[BK_PROJ][:, 0:QKV], xnt[:, n.par, k, WINDOW:KEYS], wqkv_s[:, k, :], start=(k == 0), stop=(k == KD - 1))
                    for k in range(KD):
                        last = mm(banks[BK_PROJ][:, QKV:QKV + NKV * HD], xnt[:, n.par, k, 0:P], wqkv_s[:, k, NQK * HD:QKV],
                                  start=(k == 0), stop=(k == KD - 1))
                    last.then_inc(s_proj, 1)
                n = t + (-3)
                if live(j, 3):
                    pe.wait_ge(s_att, n.times(1, 1))
                    for k in range(KD):
                        last = mm(banks[BK_PV][:, 0:D], attnt[:, P * k:P * (k + 1)], wo_s[:, k, :], start=(k == 0), stop=(k == KD - 1))
                    last.then_inc(s_wo, 1)
                n = t + (-2)
                if live(j, 2):
                    pe.wait_ge(s_ms, n.times(2, 2))
                    tr(banks[BK_S][0:4 * NPAIR, 0:P], ms[:].rearrange("p a b c -> p (a b c)"), ident).then_inc(s_mtr, 1)
                n = t + (-4)
                if live(j, 4):
                    pe.wait_ge(s_h32, n.times(2, 2))
                    if live(j, 2):
                        pe.wait_ge(s_mt, (t + (-2)).times(1, 1))
                    elif live(j, 3):
                        pe.wait_ge(s_att, (t + (-3)).times(1, 1))
                    for k in range(KD):
                        last = mm(banks[BK_S][:, 0:NE], h32[:, P * k:P * (k + 1)], gw_s[:, k, :], start=(k == 0), stop=(k == KD - 1))
                    last.then_inc(s_lg, 1)
                m, q = t + (-2), t + (-1)
                if live(j, 2):
                    pe.wait_ge(s_md, m.times(64, 64))
                    tpass(m, j, 0, j == 2)
                    tpass(m, j, 1, j == 2)
                    if after(j, 2):
                        pe.wait_ge(s_x1, m.times(1))
                if live(j, 1):
                    pe.wait_ge(s_qklo, q.times(2, 2))
                for i in range(3):
                    if live(j, 1):
                        qktr(q, j, i)
                    if live(j, 2):
                        values(m, i)
                        if i < 2:
                            tpass(m, j, i + 2, False)
                if live(j, 2):
                    values(m, 3)

            turns(pe, body)

            def wmat(at, n_):
                return w_hi[:, at:at + n_], w_lo[:, at:at + n_]

            def three(bank, whi, wlo, rhi, rlo, start, stop):
                mm(bank, whi, rhi, start=start, stop=False)
                mm(bank, whi, rlo, start=False, stop=False)
                return mm(bank, wlo, rhi, start=False, stop=stop)

            pe.sem_inc(s_afree, 2)
            pe.wait_ge(s_h2lo, NT)
            pe.wait_ge(s_wlo, NT)
            pe.wait_ge(s_lgr, NT)
            pe.wait_ge(s_x1, NT)
            pe.wait_ge(s_v, NT)

            def spread(ci, i):
                pe.wait_ge(s_wsl, ci * NE + (i - 1))
                if i == 2:
                    pe.wait_ge(s_fin, ci * 2 + 2)
                e = i - 2
                mm(banks[BK_WB][:], bc(cb_s[:, B_SEL + e], 1, P), wt[:, bass.ds(ci * CH, CH)], start=True, stop=True).then_inc(s_wb, 1)

            def gate_up(ci, i):
                nn = ci * NF + i
                for which, bank, sf, sd in ((0, BK_G, s_sl, s_g), (1, BK_U, s_a, s_u)):
                    pe.wait_ge(sf, nn + 1)
                    for k in range(KD):
                        whi, wlo = wmat(i * GU + (2 * k + which) * F, F)
                        last = three(banks[bank + i % 2][:], whi, wlo, h2_hi[:, k, bass.ds(ci * CH, CH)],
                                     h2_lo[:, k, bass.ds(ci * CH, CH)], k == 0, k == KD - 1)
                    last.then_inc(sd, 1)

            def down(ci, i):
                nn = ci * NF + i
                pe.wait_ge(s_alo, nn + 1)
                for k in range(KD):
                    whi, wlo = wmat(DOWN0 + i * D + P * k, P)
                    last = three(banks[BK_Y + k][:], whi, wlo, a_hi[i % 2], a_lo[i % 2], i == 0, i == NF - 1)
                last.then_inc(s_afree, 1)

            def chunk(ci):
                for i in range(NF):
                    if i >= 2:
                        spread(ci, i)
                    gate_up(ci, i)
                    if i == 1:
                        pe.wait_ge(s_yt, ci * 2 + 2)
                    if i >= 1:
                        down(ci, i - 1)
                down(ci, NF - 1)
                finish(ci)

            def finish(ci):
                for pr in range(2):
                    pe.wait_ge(s_yt, ci * 2 + 4)
                    if pr == 0:
                        pe.wait_ge(s_wsl, ci * NE + (NE + 1))
                    for tt in range(2):
                        for k in range(KD):
                            c0 = (2 * pr + tt) * P
                            last = tr(banks[BK_YT + pr][:, D * tt + P * k:D * tt + P * (k + 1)], yt[:, k, c0:c0 + P], ident)
                    last.then_inc(s_ytr, 1)

            pe.wait_ge(s_r, routing_steps[0])
            for i in range(2):
                if i:
                    pe.wait_ge(s_wt, 2)
                b = banks[7][0:48, :].bitcast(BF16)
                for q in range(8):
                    tt = 8 * i + q
                    last = tr(b[:, P * q:P * (q + 1)], w_parts[:, tt, :, :].rearrange("p q e -> p (q e)"), identb)
                last.then_inc(s_wtr, 1)
            pe.wait_ge(s_wt, 3)
            with pe.Fori(0, NC) as ci:
                chunk(ci)


def _consts():
    import numpy as np
    cf = np.zeros((P, NCF), np.float32)
    cf[:, C_ID:C_ID + P] = np.eye(P)
    inv = (1.0 / 10000.0 ** (np.arange(0, HD, 2) / HD)).astype(np.float32)
    ang = np.arange(S, dtype=np.float32)[:, None] * inv[None, :]
    cos, sin = np.cos(ang.astype(np.float64)), np.sin(ang.astype(np.float64))
    c2 = np.repeat(cos, 2, axis=1).reshape(NT, P, HD).transpose(1, 0, 2)
    s2 = np.stack([-sin, sin], axis=-1).reshape(NT, P, HD).transpose(1, 0, 2)
    cf[:, C_COS:C_COS + NT * HD] = c2.reshape(P, -1)
    cf[:, C_SIN:C_SIN + NT * HD] = s2.reshape(P, -1)
    a = np.arange(NGRP)
    cf[:, C_TRI:C_TRI + 16] = (a[None, :] < a[:, None]).astype(np.float32).reshape(1, 16)
    cf[:, C_NHALF] = -0.5
    cb = np.zeros((P, NCB), np.float32)
    cb[:, B_ID:B_ID + P] = np.eye(P)
    i, j = np.arange(P)[:, None], np.arange(KEYS)[None, :]
    ok = (j >= i) & (j <= i + WINDOW)
    cb[:, B_MQ:B_MQ + KEYS] = np.where(ok, 0, NEG)
    cb[:, B_MQ0:B_MQ0 + KEYS] = np.where(ok & (j >= WINDOW), 0, NEG)
    kk, q = np.arange(P)[:, None], np.arange(BLK)[None, :]
    ok = (kk >= q) & (kk <= q + WINDOW)
    cb[:, B_MT:B_MT + BLK] = np.where(ok, 0, NEG)
    cb[:, B_MT0:B_MT0 + BLK] = np.where(ok & (kk >= BLK), 0, NEG)
    for e in range(NE):
        for part in range(3):
            cb[part * NE + e, B_SEL + e] = 1
    return cf, cb


def kernel(L0_attn_x, L0_attn_rms_w, L0_attn_wq, L0_attn_wk, L0_attn_wv, L0_attn_wo, L0_ffn_gate_weight,
           L0_ffn_e_score_correction_bias, L0_ffn_gate_w, L0_ffn_up_w, L0_ffn_down_w, L0_ffn_sh_gate_w,
           L0_ffn_sh_up_w, L0_ffn_sh_down_w, L0_c, L0_wmod):
    import numpy as np
    import concourse.bacc as bacc
    from concourse.bass_utils import run_bass_kernel_spmd

    A = np.asarray
    gw = np.concatenate([A(L0_ffn_sh_gate_w).reshape(2, F, D), A(L0_ffn_gate_w)])
    uw = np.concatenate([A(L0_ffn_sh_up_w).reshape(2, F, D), A(L0_ffn_up_w)])
    gu = np.stack([gw, uw]).reshape(2, NF, F, KD, P).transpose(4, 1, 3, 0, 2).reshape(P, NF * GU)
    dw = np.concatenate([A(L0_ffn_sh_down_w).reshape(D, 2, F).transpose(1, 0, 2), A(L0_ffn_down_w)])
    dn = dw.transpose(2, 0, 1).reshape(P, NF * D)
    wbig = np.concatenate([gu, dn], axis=1).reshape(P, NT, WCH).transpose(1, 0, 2)
    cf, cb = _consts()
    arrays = {
        "x": A(L0_attn_x).reshape(S, D),
        "wqkv": np.concatenate([A(L0_attn_wq), A(L0_attn_wk), A(L0_attn_wv)], axis=1),
        "wo": A(L0_attn_wo), "rms_w": A(L0_attn_rms_w).reshape(KD, P).T, "gate_weight": A(L0_ffn_gate_weight).T,
        "bias": A(L0_ffn_e_score_correction_bias), "wbig": wbig, "c": A(L0_c).reshape(KD, P).T, "wmod": A(L0_wmod),
        "cf": cf, "cb": cb,
    }
    nc = bacc.Bacc("TRN2", target_bir_lowering=False, num_devices=1)
    ins, args = {}, []
    for name, a in arrays.items():
        a = np.ascontiguousarray(a)
        ins[f"in_{name}"] = a
        args.append(nc.dram_tensor(f"in_{name}", a.shape, mybir.dt.from_np(a.dtype), kind="ExternalInput").ap())
    args.append(nc.dram_tensor("out_0", (S, D), F32, kind="ExternalOutput").ap())
    build(nc, *args)
    r = run_bass_kernel_spmd(nc, [ins], core_ids=[0])
    return r.results[0]["out_0"].reshape(1, S, D)
```

```python
from contextlib import ExitStack

import concourse.bass as bass
from concourse import mybir

F32 = mybir.dt.float32
F32R = mybir.dt.float32r
BF16 = mybir.dt.bfloat16
ALU = mybir.AluOpType
ACT = mybir.ActivationFunctionType
AX = mybir.AxisListType

P = 128
S = 2048
D = 256
KD = D // P
NH, NKV, HD = 16, 4, 16
WINDOW = 64
NQK = NH + NKV
QKV = (NH + 2 * NKV) * HD
NT = S // P
KEYS = P + WINDOW
BLK = 64
NPAIR = NH // 2
KPAIR = NKV // 2
SLOT = 64
NE, TOPK, NGRP, TOPG, EPG = 16, 4, 4, 2, 4
ROUTED_SCALE = 2.5
F = 128
NF = NE + 2
CH = 512
NC = S // CH
TPC = CH // P
GU = KD * 2 * F
WCOLS = NF * GU + NF * D
WCH = WCOLS // NT
DOWN0 = NF * GU
NEG = -3.0e38
SCALE = HD ** -0.5
LN_EPS, RMS_EPS = 1e-5, 1e-6

C_ID, C_COS, C_SIN, C_TRI, C_NHALF = 0, P, P + NT * HD, P + 2 * NT * HD, P + 2 * NT * HD + 16
NCF = C_NHALF + 1
B_ID, B_MQ, B_MQ0, B_MT, B_MT0, B_SEL = 0, P, P + KEYS, P + 2 * KEYS, P + 2 * KEYS + BLK, P + 2 * KEYS + 2 * BLK
NCB = B_SEL + NE

BK_T, BK_PROJ, BK_S, BK_PV, BK_RING = 0, 1, 2, 3, 4
USES = "Q0 Q1 K2 T0 T1 M0 M1 T2 M2 M3 T3 M4 M5 M6 M7".split()
TR_USE = [USES.index(u) for u in ("Q0", "Q1", "K2")]
MAX_USE = [USES.index(f"M{i}") for i in range(NPAIR)]
T_USE = [USES.index(f"T{i}") for i in range(4)]


class Tile:

    def __init__(self, m, d):
        self.m, self.d, self.par = m, d, d % 2

    def __add__(self, k):
        return Tile(self.m, self.d + k)

    def times(self, per, extra=0):
        return self.m * (2 * per) + (per * self.d + extra)

    def half(self, per, extra=0):
        return self.m * per + (per * (self.d // 2) + extra)

    def static(self):
        return isinstance(self.m, int)

    def index(self):
        return self.times(1)


def bc(ap, at, n):
    dims = [list(x) for x in ap.ap]
    dims.insert(at, [0, n])
    return bass.AP(ap.tensor, ap.offset, dims)


def build(nc, x, wqkv, wo, rms_w, gate_weight, bias, wbig, c, wmod, cf, cb, out):
    x1_dram = nc.dram_tensor("x1_scratch", (S, D), F32, kind="Internal").ap()
    with ExitStack() as ctx:
        def sb(name, shape, dt=F32):
            return ctx.enter_context(nc.sbuf_tensor(name, shape, dt))

        def sem(name):
            return ctx.enter_context(nc.semaphore(name))

        banks = [ctx.enter_context(nc.psum_tensor(f"bank{i}", [P, 512], F32)) for i in range(8)]

        w_hi = sb("w_hi", [P, WCOLS], F32R)
        w_lo = sb("w_lo", [P, WCOLS], F32R)
        w_stage = sb("w_stage", [P, WCH])
        wqkv_s = sb("wqkv_s", [P, KD, QKV])
        wo_s = sb("wo_s", [P, KD, D])
        gw_s = sb("gw_s", [P, KD, NE])
        bias_s = sb("bias_s", [P, NE])
        rms_s = sb("rms_s", [P, KD])
        cf_s = sb("cf_s", [P, NCF])
        cb_s = sb("cb_s", [P, NCB], BF16)
        mod_rows = sb("mod_rows", [P, 2, D])
        mod_cols = sb("mod_cols", [P, 6])
        silu_c = sb("silu_c", [P, 4, KD])
        c_wide = sb("c_wide", [P, KD, P])
        h2_hi = sb("h2_hi", [P, KD, S], F32R)
        h2_lo = sb("h2_lo", [P, KD, S], F32R)
        xs = sb("xs", [P, 4, D])
        x1_o = sb("x1_o", [P, 2, D])
        scratch = sb("scratch", [P, 3072])
        qt = sb("qt", [P, 2, NPAIR, P], F32R)
        kt = sb("kt", [P, 2, KPAIR, KEYS], F32R)
        qs = sb("qs", [P, NH, SLOT])
        ks = sb("ks", [P, NKV, SLOT])
        xv = sb("xv", [P, S // 2])
        xnt = xv[:, 0:2 * KD * P].rearrange("p (s k t) -> p s k t", s=2, k=KD)
        vv = xv[:, 2 * KD * P:2 * KD * P + 4 * NKV * (HD + 1)].rearrange("p (s w g d) -> p s w g d", s=2, w=2, g=NKV)
        rt = sb("rt", [P, 7, D])
        logits = sb("logits", [P, NT, NE])
        wt = xv[:, 0:S // 2].bitcast(BF16)
        stat = sb("stat", [P, 2, 6])
        mv = sb("mv", [P, 2, 2])
        tiny = sb("tiny", [P, 9])
        mx = sb("mx", [P, 2, NPAIR])
        ms = sb("ms", [P, 2, 2, NPAIR])
        cb_stage = rt[:, 0:3, :].rearrange("p a b -> p (a b)")[:, 0:NCB]
        rden = sb("rden", [P, NH])
        gtmp = w_stage[:, 0:NT * 28]

        ident = cf_s[:, C_ID:C_ID + P]
        identb = cb_s[:, B_ID:B_ID + P]
        pt = [scratch[:, 512 * i:512 * i + 512] for i in range(2)]
        rope_a = scratch[:, 1024:1344]
        rope_b = scratch[:, 1344:1664]
        rope_o = scratch[:, 1664:1984]
        mt = sb("mt", [4 * NPAIR, P], F32R)
        z, h, xn, attn, attnt, z2, h32 = (rt[:, i, :] for i in range(7))
        xa = [xs[:, 0, :], xs[:, 1, :]]
        xb = [xs[:, 2, :], xs[:, 3, :]]
        ve, rstd, ssq, msq, rrms, ve2, rstd2 = (tiny[:, i:i + 1] for i in range(7))
        nhalf = cf_s[:, C_NHALF:C_NHALF + 1]
        wmod_s = scratch[:, :].rearrange("p (k n) -> p k n", k=KD)

        s_const = sem("consts_loaded")
        s_wmod = sem("wmod_loaded")
        s_small = sem("small_weights_loaded")
        s_su = sem("setup_step")
        s_su_act = sem("setup_exp")
        s_modp = sem("mod_product")
        s_ones = sem("fixed_parts_written")
        s_xa = [sem("xa_loaded0"), sem("xa_loaded1")]
        s_xb = [sem("xb_loaded0"), sem("xb_loaded1")]
        s_st = sem("ln1_stats")
        s_ag = sem("ln1_aggregated")
        s_ve = sem("ln1_variance")
        s_rstd = sem("ln1_rstd")
        s_z = sem("ln1_normal")
        s_hm = sem("h_scaled")
        s_h = sem("h_ready")
        s_ssq = sem("h_squares")
        s_msq = sem("h_mean_square")
        s_rrms = sem("h_rrms")
        s_xn = sem("xn_ready")
        s_xtr = sem("xn_transposed")
        s_xnt = sem("xnt_ready")
        s_proj = sem("projected")
        s_v = sem("v_ready")
        s_vw = [sem("v_shifted0"), sem("v_shifted1")]
        s_ra = sem("rope_products")
        s_ro = sem("rope_done")
        s_qkhi = sem("qk_high")
        s_qklo = sem("qk_low")
        s_qktr = sem("qk_transposed")
        s_qkt = sem("qkt_ready")
        s_sc = sem("scores_for_max")
        s_mxr = sem("max_read")
        s_ms = sem("max_parts")
        s_mtr = sem("max_transposed")
        s_mt = sem("max_rows_ready")
        s_md = sem("max_rows_placed")
        s_ts = sem("scores_transposed")
        s_ex = sem("probs_ready")
        s_pv = sem("weighted_values")
        s_rd = sem("denominator_inverted")
        s_at = sem("attn_ready")
        s_atr = sem("attn_transposed")
        s_att = sem("attnt_ready")
        s_wo = sem("attn_projected")
        s_x1 = sem("x1_ready")
        s_x1s = [sem("x1_stored0"), sem("x1_stored1")]
        s_st2 = sem("ln2_stats")
        s_ag2 = sem("ln2_aggregated")
        s_ve2 = sem("ln2_variance")
        s_rstd2 = sem("ln2_rstd")
        s_z2 = sem("z2_ready")
        s_z2tr = sem("z2_transposed")
        s_h32 = sem("h2_ready")
        s_h2hi = sem("h2_high")
        s_h2lo = sem("h2_low")
        s_lg = sem("logits_product")
        s_lgr = sem("logits_read")
        s_wl = sem("w_chunk_loaded")
        s_whi = sem("w_chunk_high")
        s_wlo = sem("w_chunk_low")

        s_r = sem("routing_step")
        s_rexp = sem("routing_exp")
        s_wtr = sem("weights_transposed")
        s_wt = sem("weights_row_ready")
        s_g = sem("gate_product")
        s_u = sem("up_product")
        s_wb = sem("expert_weight_spread")
        s_sl = sem("silu_ready")
        s_wsl = sem("weighted_silu_ready")
        s_a = sem("act_ready")
        s_ahi = sem("act_high")
        s_alo = sem("act_low")
        s_afree = sem("act_slot_free")
        s_yt = sem("ffn_scaled")
        s_ytr = sem("ffn_transposed")
        s_fin = sem("out_ready")
        s_x1l = sem("x1_chunk_loaded")
        s_out = [sem("out_stored0"), sem("out_stored1")]

        routing_steps = []
        w_parts = qs[:, 0:12, :].rearrange("p a b -> p (a b)").bitcast(BF16)[:, 0:NT * 48].rearrange("p (t q e) -> p t q e", q=3, e=NE)

        BK_G, BK_U, BK_Y, BK_WB, BK_YT = 0, 2, 4, 6, 6
        sl = [scratch[:, 0:512], scratch[:, 512:1024]]
        aa = [scratch[:, 1024:1536], scratch[:, 1536:2048]]
        wsl = scratch[:, 2048:2560]
        a_hi = [qt[:, 0, 4 * i:4 * i + 4, :].rearrange("p a b -> p (a b)") for i in range(2)]
        a_lo = [qt[:, 1, 4 * i:4 * i + 4, :].rearrange("p a b -> p (a b)") for i in range(2)]
        yt = qs[:].rearrange("p a b -> p (a b)").rearrange("p (k t) -> p k t", k=KD)

        def ytok(pr):
            return x1_o[:, :, :] if pr == 0 else vtok

        vtok = scratch[:, 2560:3072].rearrange("p (t d) -> p t d", t=2)

        sq_junk = scratch[:, 2048:2304]
        ks2 = bass.AP(ks[:].tensor, ks[:].offset, [list(ks[:].ap[0]), [SLOT, NKV], [2 * HD, 2], [1, HD]]).bitcast(F32R)
        SETUP_STEPS = 19

        block = ctx.enter_context(nc.Block())

        LAST = 4

        def turns(eng, body):
            for j in range(LAST):
                body(Tile(0, j), j)
            with eng.Fori(LAST // 2, NT // 2) as m:
                for k in range(2):
                    body(Tile(m, k), None)
            for j in range(NT, NT + LAST):
                body(Tile(0, j), j)

        def live(j, lag):
            return j is None or 0 <= j - lag < NT

        def after(j, lag, back=1):
            return j is None or j - lag - back >= 0

        def shifted(t):
            return t.half(32, 16 if t.par == 0 else 32)

        def ring(u):
            return banks[BK_RING + u % 4]

        @block.sync
        def _(sp):
            sp.dma_start(cf_s[:], cf).then_inc(s_const, 16)
            sp.dma_start(cb_stage, cb).then_inc(s_const, 16)
            sp.dma_start(silu_c[:, 0, :], c).then_inc(s_const, 16)
            sp.dma_start(xa[0], x[0:P, :]).then_inc(s_xa[0], 16)
            for k in range(KD):
                sp.dma_start(wmod_s[:, k, :], wmod[P * k:P * (k + 1), :]).then_inc(s_wmod, 16)
            sp.dma_start(wqkv_s[:], wqkv.rearrange("(k p) n -> p k n", p=P)).then_inc(s_small, 16)
            sp.dma_start(wo_s[:], wo.rearrange("(k p) n -> p k n", p=P)).then_inc(s_small, 16)
            sp.dma_start(gw_s[:], gate_weight.rearrange("(k p) n -> p k n", p=P)).then_inc(s_small, 16)
            sp.dma_start(rms_s[:], rms_w).then_inc(s_small, 16)
            sp.dma_start(bias_s[:], bc(bias.rearrange("(o n) -> o n", o=1)[0, :], 0, P)).then_inc(s_small, 16)

            def body(t, j):
                if live(j, 0) and j != 0:
                    if after(j, 0, 2):
                        sp.wait_ge(s_z, t.times(1, -1))
                    sp.dma_start(xa[t.par], x[bass.ds(t.times(P), P), :]).then_inc(s_xa[t.par], 16)
                n = t + (-4)
                if live(j, 4):
                    sp.wait_ge(s_x1, n.times(1, 1))
                    sp.dma_start(x1_dram[bass.ds(n.times(P), P), :], x1_o[:, n.par, :]).then_inc(s_x1s[n.par], 16)
                if live(j, 0):
                    if after(j, 0):
                        sp.wait_ge(s_wlo, t.times(1))
                    sp.dma_start(w_stage[:], wbig[bass.ds(t.index(), 1), :, :].rearrange("o p n -> (o p) n")).then_inc(s_wl, 16)
                n = t + (-2)
                if live(j, 2):
                    sp.wait_ge(s_v, n.times(1, 1))
                    if after(j, 2):
                        sp.dma_start(vv[0:WINDOW, n.par, 1, :, :], vv[WINDOW:P, 1 - n.par, 0, :, :]).then_inc(s_vw[n.par], 16)
                    sp.dma_start(vv[WINDOW:P, n.par, 1, :, :], vv[0:P - WINDOW, n.par, 0, :, :]).then_inc(s_vw[n.par], 16)
                    if after(j, 2, 2):
                        sp.wait_ge(s_x1, n.times(1, -1))
                    sp.dma_start(xb[n.par], x[bass.ds(n.times(P), P), :]).then_inc(s_xb[n.par], 16)
                    sp.wait_ge(s_mt, n.times(1, 1))
                    for hf in range(2):
                        for part in range(2):
                            r = (2 * hf + part) * NPAIR
                            row = 64 * hf + 3 * HD + part
                            sp.dma_start(qt[row:row + 1, n.par, :, :].bitcast(F32), mt[r:r + NPAIR, :].bitcast(F32)).then_inc(s_md, 16)

            turns(sp, body)
            for par in range(2):
                sp.wait_ge(s_x1s[par], 16 * NT // 2)
            for pr in range(2):
                sp.sem_inc(s_out[pr], 16)
            with sp.Fori(0, NC) as ci:
                sp.wait_ge(s_fin, ci * 2 + 2)
                sp.dma_start(xs[:], x1_dram[bass.ds(ci * CH, CH), :].rearrange("(t p) d -> p t d", p=P)).then_inc(s_x1l, 16)
                for pr in range(2):
                    sp.wait_ge(s_fin, ci * 2 + (pr + 3))
                    sp.dma_start(out[bass.ds(ci * CH + 2 * P * pr, 2 * P), :].rearrange("(t p) d -> p t d", p=P),
                                 ytok(pr)).then_inc(s_out[pr], 16)
            for pr in range(2):
                sp.wait_ge(s_out[pr], 16 * NC + 16)

        @block.gpsimd
        def _(pool):
            g = nc.gpsimd
            pool.wait_ge(s_const, 48)

            def body(t, j):
                if live(j, 0):
                    pool.wait_ge(s_ve, t.times(1, 1))
                    g.tensor_tensor(rstd, ve, nhalf, ALU.pow).then_inc(s_rstd, 1)
                n = t + (-4)
                if live(j, 4):
                    pool.wait_ge(s_ve2, n.times(1, 1))
                    g.tensor_tensor(rstd2, ve2, nhalf, ALU.pow).then_inc(s_rstd2, 1)
                if live(j, 0):
                    pool.wait_ge(s_z, t.times(1, 1))
                    if j == 0:
                        pool.wait_ge(s_su, SETUP_STEPS)
                    if after(j, 0):
                        pool.wait_ge(s_xn, t.times(1))
                    g.tensor_tensor(h, z, mod_rows[:, 1, :], ALU.mult).then_inc(s_hm, 1)
                    pool.wait_ge(s_hm, t.times(1, 1))
                    g.tensor_tensor(h, h, mod_rows[:, 0, :], ALU.add).then_inc(s_h, 1)
                n = t + (-1)
                if live(j, 1):
                    pool.wait_ge(s_qkhi, n.times(2, 2))
                    o = rope_o.rearrange("p (n d) -> p n d", d=HD)
                    if after(j, 1):
                        pool.wait_ge(s_qktr, n.times(3))
                    g.tensor_tensor(qs[:, :, 2 * HD:3 * HD].bitcast(F32R), o[:, 0:NH, :], qs[:, :, 0:HD], ALU.subtract).then_inc(s_qklo, 1)
                    g.tensor_tensor(ks[:, :, HD:2 * HD].bitcast(F32R), o[:, NH:NQK, :], ks[:, :, 0:HD], ALU.subtract).then_inc(s_qklo, 1)
                if live(j, 0):
                    pool.wait_ge(s_msq, t.times(1, 1))
                    g.tensor_tensor(rrms, msq, nhalf, ALU.pow).then_inc(s_rrms, 1)
                    pool.wait_ge(s_whi, t.times(1, 1))
                    pool.wait_ge(s_const, 48)
                    at = t.times(WCH)
                    g.tensor_tensor(w_lo[:, bass.ds(at, WCH)], w_stage[:], w_hi[:, bass.ds(at, WCH)].bitcast(F32), ALU.subtract).then_inc(s_wlo, 1)
            turns(pool, body)

        @block.vector
        def _(dve):
            v = nc.vector
            step = [0]

            def chain(ins, sem_=s_su):
                step[0] += 1
                ins.then_inc(sem_, 1)
                dve.wait_ge(sem_, step[0])

            v.memset(qs[:], 0.0).then_inc(s_ones, 1)
            v.memset(ks[:], 0.0).then_inc(s_ones, 1)
            v.memset(kt[:, 0, :, 0:WINDOW].bitcast(F32), 0.0).then_inc(s_ones, 1)
            v.memset(vv, 1.0).then_inc(s_ones, 1)
            dve.wait_ge(s_ones, 4)
            v.memset(ks[:, :, 3 * HD:3 * HD + 2], -1.0).then_inc(s_ones, 1)

            dve.wait_ge(s_const, 48)
            v.tensor_copy(cb_s[:], cb_stage).then_inc(s_ones, 1)
            dve.wait_ge(s_su_act, 1)
            chain(v.tensor_scalar(silu_c[:, 2, :], silu_c[:, 1, :], 1.0, None, ALU.add))
            chain(v.reciprocal(silu_c[:, 3, :], silu_c[:, 2, :]))
            chain(v.tensor_tensor(silu_c[:, 1, :], silu_c[:, 0, :], silu_c[:, 3, :], ALU.mult))
            chain(v.tensor_copy(c_wide[:], bc(silu_c[:, 1, :], 2, P)))
            dve.wait_ge(s_modp, 1)
            chain(v.tensor_copy(mod_rows[:, 0, :], banks[4][:, 0:D]))
            chain(v.tensor_scalar(mod_rows[:, 1, :], banks[4][:, D:2 * D], 1.0, None, ALU.add))
            chain(v.tensor_copy(mod_cols[:], banks[6][:, 0:6]))
            chain(v.tensor_scalar(mod_cols[:, 2:4], mod_cols[:, 2:4], 1.0, None, ALU.add))

            def gate(g, mag, sgn, to):
                chain(v.tensor_copy(sgn, g))
                chain(v.scalar_tensor_tensor(mag, sgn, -1.0, sgn, ALU.mult, ALU.max))
                chain(v.tensor_scalar(mag, mag, 0.25, None, ALU.max))
                chain(v.tensor_scalar(sgn, g, 0.0, 2.0, ALU.is_ge, ALU.mult))
                return v.scalar_tensor_tensor(to, sgn, -1.0, mag, ALU.add, ALU.mult)

            chain(gate(banks[5][:, 0:D], attn, attnt, z2))
            chain(gate(mod_cols[:, 4:6], tiny[:, 0:2], tiny[:, 2:4], mod_cols[:, 4:6]))
            dve.wait_ge(s_small, 80)
            chain(v.tensor_tensor(wo_s[:], wo_s[:], bc(z2, 1, KD), ALU.mult))
            for k in range(KD):
                ins = v.tensor_scalar(wqkv_s[:, k, :], wqkv_s[:, k, :], rms_s[:, k:k + 1], None, ALU.mult)
                ins.then_inc(s_ones, 1)
            assert step[0] == SETUP_STEPS, step[0]

            def maxima(t, parts):
                for q in parts:
                    a, hf = q // 2, q % 2
                    dve.wait_ge(s_sc, t.times(8, q + 1))
                    v.tensor_reduce(mx[:, hf, 2 * a:2 * a + 2],
                                    ring(MAX_USE[q])[:, 0:2 * KEYS].rearrange("p (h k) -> p h k", h=2),
                                    AX.X, ALU.max).then_inc(s_mxr, 1)

            def body(t, j):
                n = t + (-4)
                if live(j, 4):
                    dve.wait_ge(s_wo, n.times(1, 1))
                    dve.wait_ge(s_xb[n.par], n.half(16, 16))
                    if after(j, 4, 2):
                        dve.wait_ge(s_x1s[n.par], n.half(16))
                    v.tensor_tensor(x1_o[:, n.par, :], banks[BK_PV][:, 0:D], xb[n.par], ALU.add).then_inc(s_x1, 1)
                    dve.wait_ge(s_x1, n.times(1, 1))
                    v.bn_stats(stat[:, 1, :], x1_o[:, n.par, :]).then_inc(s_st2, 1)
                if live(j, 0):
                    dve.wait_ge(s_xa[t.par], t.half(16, 16))
                    v.bn_stats(stat[:, 0, :], xa[t.par]).then_inc(s_st, 1)
                if live(j, 4):
                    dve.wait_ge(s_st2, n.times(1, 1))
                    v.tensor_copy(tiny[:, 7:8], stat[:, 1, 0:1])
                    v.bn_aggr(mv[:, 1, :], stat[:, 1, :]).then_inc(s_ag2, 1)
                if live(j, 0):
                    dve.wait_ge(s_st, t.times(1, 1))
                    v.tensor_copy(tiny[:, 8:9], stat[:, 0, 0:1])
                    v.bn_aggr(mv[:, 0, :], stat[:, 0, :]).then_inc(s_ag, 1)
                if live(j, 4):
                    dve.wait_ge(s_ag2, n.times(1, 1))
                    v.tensor_scalar(ve2, mv[:, 1, 1:2], LN_EPS, None, ALU.add).then_inc(s_ve2, 1)
                if live(j, 0):
                    dve.wait_ge(s_ag, t.times(1, 1))
                    v.tensor_scalar(ve, mv[:, 0, 1:2], LN_EPS, None, ALU.add).then_inc(s_ve, 1)
                c_ = t + (-2)
                if live(j, 2):
                    if after(j, 2):
                        dve.wait_ge(s_ms, c_.times(2))
                    maxima(c_, range(2))
                if live(j, 0):
                    dve.wait_ge(s_rstd, t.times(1, 1))
                    if after(j, 0):
                        dve.wait_ge(s_h, t.times(1))
                    v.tensor_scalar(z, xa[t.par], mv[:, 0, 0:1], rstd, ALU.subtract, ALU.mult).then_inc(s_z, 1)
                if live(j, 4):
                    dve.wait_ge(s_rstd2, n.times(1, 1))
                    if after(j, 4):
                        dve.wait_ge(s_z2tr, n.times(1))
                    v.tensor_scalar(z2, x1_o[:, n.par, :], mv[:, 1, 0:1], rstd2, ALU.subtract, ALU.mult).then_inc(s_z2, 1)
                if live(j, 2):
                    maxima(c_, range(2, 4))
                n = t + (-1)
                if live(j, 1):
                    dve.wait_ge(s_proj, n.times(1, 1))
                    src = banks[BK_PROJ][:, 0:NQK * HD].rearrange("p (n d) -> p n d", d=HD)
                    sw = bass.AP(src.tensor, src.offset + 1, [list(src.ap[0]), [HD, NQK], [2, HD // 2], [-1, 2]])
                    cos = bc(cf_s[:, bass.ds(n.times(HD, C_COS), HD)], 1, NQK)
                    sin = bc(cf_s[:, bass.ds(n.times(HD, C_SIN), HD)].rearrange("p (i j) -> p i j", j=2), 1, NQK)
                    v.tensor_tensor(rope_a.rearrange("p (n d) -> p n d", d=HD), src, cos, ALU.mult).then_inc(s_ra, 1)
                    v.tensor_tensor(rope_b.rearrange("p (n i j) -> p n i j", i=HD // 2, j=2), sw, sin, ALU.mult).then_inc(s_ra, 1)
                if live(j, 2):
                    maxima(c_, range(4, 5))
                if live(j, 1):
                    dve.wait_ge(s_ra, n.times(2, 2))
                    if after(j, 1):
                        dve.wait_ge(s_qklo, n.times(2))
                    v.tensor_tensor(rope_o, rope_a, rope_b, ALU.add).then_inc(s_ro, 1)
                if live(j, 2):
                    maxima(c_, range(5, 6))
                if live(j, 0):
                    dve.wait_ge(s_ssq, t.times(1, 1))
                    v.tensor_scalar(msq, ssq, 1.0 / D, RMS_EPS, ALU.mult, ALU.add).then_inc(s_msq, 1)
                n = t + (-4)
                if live(j, 4):
                    dve.wait_ge(s_z2tr, n.times(1, 1))
                    if after(j, 4):
                        dve.wait_ge(s_lg, n.times(1))
                    for k in range(KD):
                        v.tensor_scalar(h32[:, P * k:P * (k + 1)], banks[BK_T][:, P * k:P * (k + 1)],
                                        mod_cols[:, 2 + k:3 + k], mod_cols[:, k:k + 1],
                                        ALU.mult, ALU.add).then_inc(s_h32, 1)
                if live(j, 2):
                    maxima(c_, range(6, 8))
                    dve.wait_ge(s_mxr, c_.times(8, 8))
                    if after(j, 2):
                        dve.wait_ge(s_mtr, c_.times(1))
                    v.tensor_copy(ms[:, :, 0, :].bitcast(F32R), mx[:]).then_inc(s_ms, 1)
                    dve.wait_ge(s_ms, c_.times(2, 1))
                    v.tensor_tensor(ms[:, :, 1, :].bitcast(F32R), mx[:], ms[:, :, 0, :], ALU.subtract).then_inc(s_ms, 1)
                if live(j, 0):
                    dve.wait_ge(s_rrms, t.times(1, 1))
                    if after(j, 0):
                        dve.wait_ge(s_xtr, t.times(1))
                    v.tensor_scalar(xn, h, rrms, None, ALU.mult).then_inc(s_xn, 1)
                h3 = h32.rearrange("p (k t) -> p k t", k=KD)
                at = bass.ds(n.times(P), P)
                if live(j, 4):
                    dve.wait_ge(s_h32, n.times(2, 2))
                    v.tensor_scalar(h2_hi[:, :, at], h3, 1.0, None, ALU.mult).then_inc(s_h2hi, 1)
                d_ = t + (-3)
                if live(j, 3):
                    pv = banks[BK_PV][:, 0:NH * (HD + 1)].rearrange("p (h d) -> p h d", h=NH)
                    dve.wait_ge(s_pv, d_.times(4, 4))
                    v.reciprocal(rden[:], pv[:, :, HD]).then_inc(s_rd, 1)
                    dve.wait_ge(s_rd, d_.times(1, 1))
                    if after(j, 3):
                        dve.wait_ge(s_atr, d_.times(1))
                    v.tensor_tensor(attn.rearrange("p (h d) -> p h d", h=NH), pv[:, :, 0:HD],
                                    bc(rden[:], 2, HD), ALU.mult).then_inc(s_at, 1)
                if live(j, 4):
                    dve.wait_ge(s_lg, n.times(1, 1))
                    v.tensor_scalar(logits[:, bass.ds(n.index(), 1), :].rearrange("p o e -> p (o e)"),
                                    banks[BK_S][:, 0:NE], 1.0, None, ALU.mult).then_inc(s_lgr, 1)
                    dve.wait_ge(s_h2hi, n.times(1, 1))
                    v.tensor_tensor(h2_lo[:, :, at], h3, h2_hi[:, :, at].bitcast(F32), ALU.subtract).then_inc(s_h2lo, 1)

            turns(dve, body)

            E3 = lambda a: a.rearrange("p (t e) -> p t e", e=NE)
            G4 = lambda a: a.rearrange("p (t g e) -> p t g e", g=NGRP, e=EPG)
            ex, sc, ch, mk, rep, wgt, tmp = (rt[:, i, :] for i in range(7))
            step[0] = 0

            def link(ins):
                chain(ins, s_r)

            dve.wait_ge(s_rexp, 1)
            dve.wait_ge(s_wlo, NT)
            dve.wait_ge(s_h2lo, NT)
            link(v.tensor_scalar(tmp, ex, 1.0, None, ALU.add))
            link(v.reciprocal(sc, tmp))
            link(v.tensor_tensor(E3(ch), E3(sc), bc(bias_s[:], 1, NT), ALU.add))
            c4 = G4(ch)
            prs = gtmp[:, 0:NT * 24].rearrange("p (t g s) -> p t g s", g=NGRP, s=6)
            v.tensor_tensor(prs[:, :, :, 0:3], c4[:, :, :, 0:3], c4[:, :, :, 1:4], ALU.add)
            v.tensor_tensor(prs[:, :, :, 3:5], c4[:, :, :, 0:2], c4[:, :, :, 2:4], ALU.add)
            link(v.tensor_tensor(prs[:, :, :, 5:6], c4[:, :, :, 0:1], c4[:, :, :, 3:4], ALU.add))
            gs = gtmp[:, NT * 24:NT * 28].rearrange("p (t g) -> p t g", g=NGRP)
            link(v.tensor_reduce(gs, prs, AX.X, ALU.max))
            other, own = bc(gs, 2, NGRP), bc(gs, 3, NGRP)
            tri = bc(cf_s[:, C_TRI:C_TRI + 16].rearrange("p (a b) -> p a b", b=NGRP), 1, NT)
            v.tensor_tensor(G4(tmp), other, own, ALU.is_gt)
            link(v.tensor_tensor(G4(ex), other, own, ALU.is_equal))
            link(v.tensor_tensor(G4(ex), G4(ex), tri, ALU.mult))
            link(v.tensor_tensor(tmp, tmp, ex, ALU.add))
            rank = gtmp[:, 0:NT * NGRP].rearrange("p (t g) -> p t g", g=NGRP)
            link(v.tensor_reduce(rank, G4(tmp), AX.X, ALU.add))
            gm = gtmp[:, NT * NGRP:2 * NT * NGRP].rearrange("p (t g) -> p t g", g=NGRP)
            gn = gtmp[:, 2 * NT * NGRP:3 * NT * NGRP].rearrange("p (t g) -> p t g", g=NGRP)
            v.tensor_scalar(gm, rank, TOPG - 0.5, None, ALU.is_lt)
            link(v.tensor_scalar(gn, rank, TOPG - 0.5, NEG, ALU.is_gt, ALU.mult))
            link(v.tensor_tensor(G4(mk), G4(ch), bc(gm, 3, EPG), ALU.mult))
            link(v.tensor_tensor(G4(mk), G4(mk), bc(gn, 3, EPG), ALU.add))
            top = gtmp[:, 0:NT * 8].rearrange("p (t k) -> p t k", k=8)
            for i in range(NT):
                ins = v.max(top[:, i, :], E3(mk)[:, i, :])
            link(ins)
            link(v.memset(top[:, :, TOPK:8], 2.0e38))
            for i in range(NT):
                ins = v.match_replace(E3(rep)[:, i, :], top[:, i, :], E3(mk)[:, i, :], -NEG)
            link(ins)
            link(v.tensor_scalar(rep, rep, 1.0e38, None, ALU.is_gt))
            link(v.tensor_tensor(wgt, sc, rep, ALU.mult))
            sm = gtmp[:, 0:NT]
            link(v.tensor_reduce(sm, E3(wgt), AX.X, ALU.add))
            link(v.tensor_scalar(sm, sm, 1e-20, None, ALU.add))
            link(v.reciprocal(gtmp[:, NT:2 * NT], sm))
            link(v.tensor_tensor(E3(wgt), E3(wgt), bc(gtmp[:, NT:2 * NT], 2, NE), ALU.mult))
            link(v.tensor_scalar(wgt, wgt, ROUTED_SCALE, None, ALU.mult))
            parts = w_parts
            link(v.tensor_copy(parts[:, :, 0, :], E3(wgt)))
            link(v.tensor_tensor(E3(tmp), E3(wgt), parts[:, :, 0, :], ALU.subtract))
            link(v.tensor_copy(parts[:, :, 1, :], E3(tmp)))
            link(v.tensor_tensor(parts[:, :, 2, :], E3(tmp), parts[:, :, 1, :], ALU.subtract))
            routing_steps.append(step[0])
            v.memset(xv[:, 0:S // 2], 0.0).then_inc(s_wt, 1)
            dve.wait_ge(s_wt, 1)
            for i in range(2):
                dve.wait_ge(s_wtr, i + 1)
                v.tensor_copy(wt[0:48, 1024 * i:1024 * (i + 1)], banks[7][0:48, :].bitcast(BF16)).then_inc(s_wt, 1)

            def act_(ci, i):
                nn = ci * NF + i
                dve.wait_ge(s_u, nn + 1)
                left = sl[i % 2] if i < 2 else wsl
                if i < 2:
                    dve.wait_ge(s_sl, nn + 3)
                else:
                    dve.wait_ge(s_wsl, ci * NE + i)
                v.tensor_tensor(aa[i % 2], left, banks[BK_U + i % 2][:], ALU.mult).then_inc(s_a, 1)

            def low(ci, i):
                nn = ci * NF + i
                dve.wait_ge(s_ahi, nn + 1)
                v.tensor_tensor(a_lo[i % 2], aa[i % 2], a_hi[i % 2].bitcast(F32), ALU.subtract).then_inc(s_alo, 1)

            def weighted(ci, i):
                nn = ci * NF + i
                dve.wait_ge(s_sl, nn + 3)
                dve.wait_ge(s_wb, ci * NE + (i - 1))
                v.tensor_tensor(wsl, sl[i % 2], banks[BK_WB][:], ALU.mult).then_inc(s_wsl, 1)

            dve.sem_inc(s_a, 2)
            dve.sem_inc(s_wsl, 1)
            dve.sem_inc(s_fin, 2)
            with dve.Fori(0, NC) as ci:
                for i in range(NF):
                    act_(ci, i)
                    low(ci, i)
                    if 2 <= i + 1 < NF:
                        weighted(ci, i + 1)
                for pr in range(2):
                    dve.wait_ge(s_ytr, ci * 2 + (pr + 1))
                    if pr == 0:
                        dve.wait_ge(s_x1l, ci * 16 + 16)
                    dve.wait_ge(s_out[pr], ci * 16 + 16)
                    v.tensor_tensor(ytok(pr), banks[BK_YT + pr][:].rearrange("p (t d) -> p t d", t=2),
                                    xs[:, 2 * pr:2 * pr + 2, :], ALU.add).then_inc(s_fin, 1)

        @block.scalar
        def _(act):
            a = nc.scalar
            act.wait_ge(s_const, 48)
            a.activation(silu_c[:, 1, :], silu_c[:, 0, :], ACT.Exp, scale=-1.0).then_inc(s_su_act, 1)

            def exps(n, j, i):
                u = T_USE[i]
                act.wait_ge(s_ts, n.times(4, i + 1))
                if i >= 2 or after(j, 3):
                    act.wait_ge(s_pv, n.times(4, i - 1))
                a.activation(pt[i % 2], ring(u)[:], ACT.Exp, scale=SCALE).then_inc(s_ex, 1)

            def evac(n, j, i):
                act.wait_ge(s_qktr, n.times(3, i + 1))
                b = ring(TR_USE[i])[:, 0:P * (4 if i < 2 else KPAIR)].rearrange("p (a t) -> p a t", t=P)
                if i == 0 and after(j, 2, 2):
                    act.wait_ge(s_ts, n.times(4, -4))
                if i < 2:
                    a.activation(qt[:, n.par, 4 * i:4 * i + 4, :], b, ACT.Copy).then_inc(s_qkt, 1)
                else:
                    if after(j, 2):
                        act.wait_ge(s_qkt, n.times(4))
                        a.activation(kt[:, n.par, :, 0:WINDOW], kt[:, 1 - n.par, :, P:KEYS].bitcast(F32), ACT.Copy).then_inc(s_qkt, 1)
                    a.activation(kt[:, n.par, :, WINDOW:KEYS], b, ACT.Copy).then_inc(s_qkt, 1 if after(j, 2) else 2)

            def body(t, j):
                n = t + (-2)
                if live(j, 2):
                    for i in range(3):
                        evac(n, j, i)
                n = t + (-1)
                if live(j, 1):
                    act.wait_ge(s_xtr, n.times(1, 1))
                    if after(j, 1, 2):
                        act.wait_ge(s_proj, n.times(1, -1))
                    a.activation(xnt[:, n.par, :, :], banks[BK_T][:, 0:D].rearrange("p (k t) -> p k t", k=KD),
                                 ACT.Copy).then_inc(s_xnt, 1)
                m = t + (-3)
                if live(j, 3):
                    for i in range(3):
                        exps(m, j, i)
                if live(j, 0):
                    act.wait_ge(s_h, t.times(1, 1))
                    if after(j, 0):
                        act.wait_ge(s_msq, t.times(1))
                    a.activation(sq_junk, h, ACT.Square, accum_out=ssq).then_inc(s_ssq, 1)
                if live(j, 3):
                    exps(m, j, 3)
                if live(j, 1):
                    act.wait_ge(s_ro, n.times(1, 1))
                    if after(j, 1):
                        act.wait_ge(s_qktr, n.times(3))
                    o = rope_o.rearrange("p (n d) -> p n d", d=HD)
                    a.activation(qs[:, :, 0:2 * HD].rearrange("p h (r d) -> p h r d", r=2).bitcast(F32R),
                                 bc(o[:, 0:NH, :], 2, 2), ACT.Copy).then_inc(s_qkhi, 1)
                    a.activation(ks2, bc(o[:, NH:NQK, :], 2, 2), ACT.Copy).then_inc(s_qkhi, 1)
                if live(j, 0):
                    act.wait_ge(s_wl, t.times(16, 16))
                    act.wait_ge(s_const, 48)
                    a.activation(w_hi[:, bass.ds(t.times(WCH), WCH)], w_stage[:], ACT.Copy).then_inc(s_whi, 1)
                n = t + (-2)
                if live(j, 2):
                    act.wait_ge(s_mtr, n.times(1, 1))
                    if after(j, 2):
                        act.wait_ge(s_md, n.times(64))
                    a.activation(mt[:], banks[BK_S][0:4 * NPAIR, 0:P], ACT.Copy).then_inc(s_mt, 1)
                n = t + (-1)
                if live(j, 1):
                    act.wait_ge(s_ra, n.times(2, 2))
                    if j == 1:
                        act.wait_ge(s_ones, 8)
                    if after(j, 1, 2):
                        act.wait_ge(s_pv, n.times(4, -4))
                        act.wait_ge(s_vw[1 - n.par], shifted(n + (-1)))
                    a.activation(vv[:, n.par, 0, :, 0:HD],
                                 banks[BK_PROJ][:, NQK * HD:QKV].rearrange("p (g d) -> p g d", g=NKV),
                                 ACT.Copy).then_inc(s_v, 1)
                if live(j, 3):
                    act.wait_ge(s_atr, m.times(1, 1))
                    if after(j, 3):
                        act.wait_ge(s_wo, m.times(1))
                    a.activation(attnt, banks[BK_T][:, 0:D], ACT.Copy).then_inc(s_att, 1)

            turns(act, body)

            act.wait_ge(s_lgr, NT)
            a.activation(rt[:, 0, :], logits[:].rearrange("p t e -> p (t e)"), ACT.Exp, scale=-1.0).then_inc(s_rexp, 1)

            act.sem_inc(s_sl, 2)
            act.sem_inc(s_yt, 2)
            with act.Fori(0, NC) as ci:
                for i in range(NF + 1):
                    nn = ci * NF + i
                    if i >= 1:
                        act.wait_ge(s_a, nn + 2)
                        act.wait_ge(s_afree, nn)
                        a.activation(a_hi[(i - 1) % 2], aa[(i - 1) % 2], ACT.Copy).then_inc(s_ahi, 1)
                    if i < NF:
                        act.wait_ge(s_g, nn + 1)
                        act.wait_ge(s_a, nn + 1)
                        a.activation(sl[i % 2], banks[BK_G + i % 2][:], ACT.Silu).then_inc(s_sl, 1)
                for k in range(KD):
                    act.wait_ge(s_afree, ci * NF + (NF + 2))
                    a.activation(yt[:, k, :], banks[BK_Y + k][:], ACT.Copy, scale=mod_cols[:, 4 + k:5 + k]).then_inc(s_yt, 1)


        @block.tensor
        def _(pe):
            mm = nc.tensor.matmul
            tr = nc.tensor.transpose

            pe.wait_ge(s_su, 4)
            pe.wait_ge(s_wmod, 16 * KD)
            for bank, lo_, n_ in ((4, 0, 2 * D), (5, 2 * D, D)):
                for k in range(KD):
                    mm(banks[bank][:, 0:n_], c_wide[:, k, :], wmod_s[:, k, lo_:lo_ + n_], start=(k == 0), stop=(k == KD - 1))
            for i in range(6):
                for k in range(KD):
                    last = mm(banks[6][:, i:i + 1], wmod_s[:, k, 3 * D + P * i:3 * D + P * (i + 1)], silu_c[:, 1, k:k + 1],
                              start=(k == 0), stop=(k == KD - 1))
            last.then_inc(s_modp, 1)
            pe.wait_ge(s_ones, 8)
            pe.wait_ge(s_const, 48)
            pe.wait_ge(s_su, SETUP_STEPS)

            def free(t, j, use):
                u = USES.index(use)
                same = u >= 4
                last = USES[u - 4] if same else USES[u + 12 if u < 3 else 11]
                i = int(last[1])
                if last[0] == "M" and live(j if same or j is None else j - 1, 2):
                    c_ = t + (-2 if same else -3)
                    pe.wait_ge(s_mxr, c_.times(8, i + 1))
                elif last[0] == "T" and live(j, 3):
                    pe.wait_ge(s_ex, (t + (-3)).times(4, i + 1))
                elif last[0] in "QK" and live(j, 2):
                    pe.wait_ge(s_qkt, (t + (-2)).times(4, i + 1 if i < 2 else 4))

            def maxpass(t, j, parts):
                n = t + (-2)
                for q in parts:
                    a_, hf, b = q // 2, q % 2, ring(MAX_USE[q])
                    free(t, j, f"M{q}")
                    mq = B_MQ0 if j == 2 else B_MQ
                    mm(b[:, 0:2 * KEYS], identb, bc(cb_s[:, mq:mq + KEYS], 1, 2), start=True, stop=True)
                    if q == 0:
                        pe.wait_ge(s_qkt, n.times(4, 4))
                    for i in range(2):
                        p_ = 2 * a_ + i
                        last = mm(b[:, i * KEYS:(i + 1) * KEYS], qt[64 * hf:64 * hf + 3 * HD, n.par, p_, :],
                                  kt[64 * hf:64 * hf + 3 * HD, n.par, p_ // 4, :], start=False, stop=True, skip_group_check=True)
                    last.then_inc(s_sc, 1)

            def tpass(t, j, i):
                n = t + (-3)
                b2, hf, b = i // 2, i % 2, ring(T_USE[i])
                free(t, j, f"T{i}")
                mq = B_MT0 if j == 3 and b2 == 0 else B_MT
                mm(b[:], identb, bc(cb_s[:, mq:mq + BLK], 1, NPAIR), start=True, stop=True)
                if i == 0:
                    pe.wait_ge(s_md, n.times(64, 64))
                R = 3 * HD + 2
                for a_ in range(KPAIR):
                    last = mm(b[:, 2 * P * a_:2 * P * (a_ + 1)], kt[64 * hf:64 * hf + R, n.par, a_, BLK * b2:BLK * b2 + P],
                              qt[64 * hf:64 * hf + R, n.par, 4 * a_:4 * a_ + 4, BLK * b2:BLK * (b2 + 1)],
                              start=False, stop=True, skip_group_check=True)
                last.then_inc(s_ts, 1)

            def values(n, i):
                b2, hf = i // 2, i % 2
                pe.wait_ge(s_ex, n.times(4, i + 1))
                if i == 0:
                    pe.wait_ge(s_v, n.times(1, 1))
                    pe.wait_ge(s_vw[n.par], shifted(n))
                for p_ in range(NPAIR):
                    h_ = 2 * p_ + hf
                    last = mm(banks[BK_PV][BLK * b2:BLK * (b2 + 1), h_ * (HD + 1):(h_ + 1) * (HD + 1)],
                              pt[i % 2][:, BLK * p_:BLK * (p_ + 1)], vv[:, n.par, 1 - b2, 2 * (p_ // 4) + hf, :], start=True, stop=True)
                last.then_inc(s_pv, 1)

            def qktr(t, j, i):
                u = TR_USE[i]
                free(t, j, USES[u])
                for a_ in range(4 if i < 2 else KPAIR):
                    if i < 2:
                        p_ = 4 * i + a_
                        src = qs[:, 2 * p_:2 * p_ + 2, :].rearrange("p a b -> p (a b)")
                    else:
                        src = ks[:, 2 * a_:2 * a_ + 2, :].rearrange("p a b -> p (a b)")
                    last = tr(ring(u)[:, P * a_:P * (a_ + 1)], src, ident)
                last.then_inc(s_qktr, 1)

            def body(t, j):
                b_, c_, d_, f_ = t + (-1), t + (-2), t + (-3), t + (-4)
                if live(j, 2):
                    pe.wait_ge(s_qklo, c_.times(2, 2))
                    for i in range(3):
                        qktr(t, j, i)
                if live(j, 4):
                    pe.wait_ge(s_att, f_.times(1, 1))
                    for k in range(KD):
                        last = mm(banks[BK_PV][:, 0:D], attnt[:, P * k:P * (k + 1)], wo_s[:, k, :], start=(k == 0), stop=(k == KD - 1))
                    last.then_inc(s_wo, 1)
                if live(j, 1):
                    pe.wait_ge(s_xn, b_.times(1, 1))
                    if not live(j, 4) and after(j, 1):
                        pe.wait_ge(s_xnt, b_.times(1))
                    for k in range(KD):
                        last = tr(banks[BK_T][:, P * k:P * (k + 1)], xn[:, P * k:P * (k + 1)], ident)
                    last.then_inc(s_xtr, 1)
                if live(j, 3):
                    if j == NT + 2:
                        pe.wait_ge(s_mxr, 8 * NT)
                    tpass(t, j, 0)
                    tpass(t, j, 1)
                if live(j, 2):
                    maxpass(t, j, range(0, 2))
                if live(j, 3):
                    if after(j, 3):
                        pe.wait_ge(s_x1, d_.times(1))
                    values(d_, 0)
                    tpass(t, j, 2)
                if live(j, 2):
                    maxpass(t, j, range(2, 4))
                if live(j, 3):
                    values(d_, 1)
                    tpass(t, j, 3)
                if live(j, 1):
                    pe.wait_ge(s_xnt, b_.times(1, 1))
                    if after(j, 1):
                        pe.wait_ge(s_v, b_.times(1))
                        pe.wait_ge(s_ra, b_.times(2))
                    for k in range(KD):
                        last = mm(banks[BK_PROJ][:, 0:QKV], xnt[:, b_.par, k, :], wqkv_s[:, k, :], start=(k == 0), stop=(k == KD - 1))
                    last.then_inc(s_proj, 1)
                if live(j, 2):
                    maxpass(t, j, range(4, 6))
                if live(j, 4):
                    pe.wait_ge(s_z2, f_.times(1, 1))
                    for k in range(KD):
                        last = tr(banks[BK_T][:, P * k:P * (k + 1)], z2[:, P * k:P * (k + 1)], ident)
                    last.then_inc(s_z2tr, 1)
                if live(j, 3):
                    values(d_, 2)
                if live(j, 2):
                    maxpass(t, j, range(6, 8))
                if live(j, 3):
                    values(d_, 3)
                if live(j, 2):
                    pe.wait_ge(s_ms, c_.times(2, 2))
                    if after(j, 4):
                        pe.wait_ge(s_lgr, f_.times(1))
                    tr(banks[BK_S][0:4 * NPAIR, 0:P], ms[:].rearrange("p a b c -> p (a b c)"), ident).then_inc(s_mtr, 1)
                if live(j, 3):
                    if live(j, 4):
                        pe.wait_ge(s_h32, f_.times(2, 2))
                    pe.wait_ge(s_at, d_.times(1, 1))
                    for k in range(KD):
                        last = tr(banks[BK_T][:, P * k:P * (k + 1)], attn[:, P * k:P * (k + 1)], ident)
                    last.then_inc(s_atr, 1)
                if live(j, 4):
                    if live(j, 2):
                        pe.wait_ge(s_mt, c_.times(1, 1))
                    pe.wait_ge(s_h32, f_.times(2, 2))
                    for k in range(KD):
                        last = mm(banks[BK_S][:, 0:NE], h32[:, P * k:P * (k + 1)], gw_s[:, k, :], start=(k == 0), stop=(k == KD - 1))
                    last.then_inc(s_lg, 1)

            turns(pe, body)

            def wmat(at, n_):
                return w_hi[:, at:at + n_], w_lo[:, at:at + n_]

            def three(bank, whi, wlo, rhi, rlo, start, stop):
                mm(bank, whi, rhi, start=start, stop=False)
                mm(bank, whi, rlo, start=False, stop=False)
                return mm(bank, wlo, rhi, start=False, stop=stop)

            pe.sem_inc(s_afree, 2)
            pe.wait_ge(s_h2lo, NT)
            pe.wait_ge(s_wlo, NT)
            pe.wait_ge(s_lgr, NT)
            pe.wait_ge(s_x1, NT)
            pe.wait_ge(s_v, NT)

            def spread(ci, i):
                pe.wait_ge(s_wsl, ci * NE + (i - 1))
                if i == 2:
                    pe.wait_ge(s_fin, ci * 2 + 2)
                e = i - 2
                mm(banks[BK_WB][:], bc(cb_s[:, B_SEL + e], 1, P), wt[:, bass.ds(ci * CH, CH)], start=True, stop=True).then_inc(s_wb, 1)

            def gate_up(ci, i):
                nn = ci * NF + i
                for which, bank, sf, sd in ((0, BK_G, s_sl, s_g), (1, BK_U, s_a, s_u)):
                    pe.wait_ge(sf, nn + 1)
                    for k in range(KD):
                        whi, wlo = wmat(i * GU + (2 * k + which) * F, F)
                        last = three(banks[bank + i % 2][:], whi, wlo, h2_hi[:, k, bass.ds(ci * CH, CH)],
                                     h2_lo[:, k, bass.ds(ci * CH, CH)], k == 0, k == KD - 1)
                    last.then_inc(sd, 1)

            def down(ci, i):
                nn = ci * NF + i
                pe.wait_ge(s_alo, nn + 1)
                for k in range(KD):
                    whi, wlo = wmat(DOWN0 + i * D + P * k, P)
                    last = three(banks[BK_Y + k][:], whi, wlo, a_hi[i % 2], a_lo[i % 2], i == 0, i == NF - 1)
                last.then_inc(s_afree, 1)

            def chunk(ci):
                for i in range(NF):
                    if i >= 2:
                        spread(ci, i)
                    gate_up(ci, i)
                    if i == 1:
                        pe.wait_ge(s_yt, ci * 2 + 2)
                    if i >= 1:
                        down(ci, i - 1)
                down(ci, NF - 1)
                finish(ci)

            def finish(ci):
                for pr in range(2):
                    pe.wait_ge(s_yt, ci * 2 + 4)
                    if pr == 0:
                        pe.wait_ge(s_wsl, ci * NE + (NE + 1))
                    for tt in range(2):
                        for k in range(KD):
                            c0 = (2 * pr + tt) * P
                            last = tr(banks[BK_YT + pr][:, D * tt + P * k:D * tt + P * (k + 1)], yt[:, k, c0:c0 + P], ident)
                    last.then_inc(s_ytr, 1)

            pe.wait_ge(s_r, routing_steps[0])
            for i in range(2):
                if i:
                    pe.wait_ge(s_wt, 2)
                b = banks[7][0:48, :].bitcast(BF16)
                for q in range(8):
                    tt = 8 * i + q
                    last = tr(b[:, P * q:P * (q + 1)], w_parts[:, tt, :, :].rearrange("p q e -> p (q e)"), identb)
                last.then_inc(s_wtr, 1)
            pe.wait_ge(s_wt, 3)
            with pe.Fori(0, NC) as ci:
                chunk(ci)


def _consts():
    import numpy as np
    cf = np.zeros((P, NCF), np.float32)
    cf[:, C_ID:C_ID + P] = np.eye(P)
    inv = (1.0 / 10000.0 ** (np.arange(0, HD, 2) / HD)).astype(np.float32)
    ang = np.arange(S, dtype=np.float32)[:, None] * inv[None, :]
    cos, sin = np.cos(ang.astype(np.float64)), np.sin(ang.astype(np.float64))
    c2 = np.repeat(cos, 2, axis=1).reshape(NT, P, HD).transpose(1, 0, 2)
    s2 = np.stack([-sin, sin], axis=-1).reshape(NT, P, HD).transpose(1, 0, 2)
    cf[:, C_COS:C_COS + NT * HD] = c2.reshape(P, -1)
    cf[:, C_SIN:C_SIN + NT * HD] = s2.reshape(P, -1)
    a = np.arange(NGRP)
    cf[:, C_TRI:C_TRI + 16] = (a[None, :] < a[:, None]).astype(np.float32).reshape(1, 16)
    cf[:, C_NHALF] = -0.5
    cb = np.zeros((P, NCB), np.float32)
    cb[:, B_ID:B_ID + P] = np.eye(P)
    i, j = np.arange(P)[:, None], np.arange(KEYS)[None, :]
    ok = (j >= i) & (j <= i + WINDOW)
    cb[:, B_MQ:B_MQ + KEYS] = np.where(ok, 0, NEG)
    cb[:, B_MQ0:B_MQ0 + KEYS] = np.where(ok & (j >= WINDOW), 0, NEG)
    kk, q = np.arange(P)[:, None], np.arange(BLK)[None, :]
    ok = (kk >= q) & (kk <= q + WINDOW)
    cb[:, B_MT:B_MT + BLK] = np.where(ok, 0, NEG)
    cb[:, B_MT0:B_MT0 + BLK] = np.where(ok & (kk >= BLK), 0, NEG)
    for e in range(NE):
        for part in range(3):
            cb[part * NE + e, B_SEL + e] = 1
    return cf, cb


def kernel(L0_attn_x, L0_attn_rms_w, L0_attn_wq, L0_attn_wk, L0_attn_wv, L0_attn_wo, L0_ffn_gate_weight,
           L0_ffn_e_score_correction_bias, L0_ffn_gate_w, L0_ffn_up_w, L0_ffn_down_w, L0_ffn_sh_gate_w,
           L0_ffn_sh_up_w, L0_ffn_sh_down_w, L0_c, L0_wmod):
    import numpy as np
    import concourse.bacc as bacc
    from concourse.bass_utils import run_bass_kernel_spmd

    A = np.asarray
    gw = np.concatenate([A(L0_ffn_sh_gate_w).reshape(2, F, D), A(L0_ffn_gate_w)])
    uw = np.concatenate([A(L0_ffn_sh_up_w).reshape(2, F, D), A(L0_ffn_up_w)])
    gu = np.stack([gw, uw]).reshape(2, NF, F, KD, P).transpose(4, 1, 3, 0, 2).reshape(P, NF * GU)
    dw = np.concatenate([A(L0_ffn_sh_down_w).reshape(D, 2, F).transpose(1, 0, 2), A(L0_ffn_down_w)])
    dn = dw.transpose(2, 0, 1).reshape(P, NF * D)
    wbig = np.concatenate([gu, dn], axis=1).reshape(P, NT, WCH).transpose(1, 0, 2)
    heads = np.arange(NH).reshape(2, NPAIR).T.reshape(-1)
    kv = np.arange(NKV).reshape(2, KPAIR).T.reshape(-1)
    wq, wk, wv = (A(w).reshape(D, -1, HD)[:, o].reshape(D, -1)
                  for w, o in ((L0_attn_wq, heads), (L0_attn_wk, kv), (L0_attn_wv, kv)))
    wo = A(L0_attn_wo).reshape(NH, HD, D)[heads].reshape(D, D)
    cf, cb = _consts()
    arrays = {
        "x": A(L0_attn_x).reshape(S, D),
        "wqkv": np.concatenate([wq, wk, wv], axis=1),
        "wo": wo, "rms_w": A(L0_attn_rms_w).reshape(KD, P).T, "gate_weight": A(L0_ffn_gate_weight).T,
        "bias": A(L0_ffn_e_score_correction_bias), "wbig": wbig, "c": A(L0_c).reshape(KD, P).T, "wmod": A(L0_wmod),
        "cf": cf, "cb": cb,
    }
    nc = bacc.Bacc("TRN2", target_bir_lowering=False, num_devices=1)
    ins, args = {}, []
    for name, a in arrays.items():
        a = np.ascontiguousarray(a)
        ins[f"in_{name}"] = a
        args.append(nc.dram_tensor(f"in_{name}", a.shape, mybir.dt.from_np(a.dtype), kind="ExternalInput").ap())
    args.append(nc.dram_tensor("out_0", (S, D), F32, kind="ExternalOutput").ap())
    build(nc, *args)
    r = run_bass_kernel_spmd(nc, [ins], core_ids=[0])
    return r.results[0]["out_0"].reshape(1, S, D)
```

```python
from contextlib import ExitStack

import concourse.bass as bass
from concourse import mybir

F32 = mybir.dt.float32
F32R = mybir.dt.float32r
BF16 = mybir.dt.bfloat16
ALU = mybir.AluOpType
ACT = mybir.ActivationFunctionType
AX = mybir.AxisListType

P = 128
S = 2048
D = 256
KD = D // P
NH, NKV, HD = 16, 4, 16
WINDOW = 64
NQK = NH + NKV
QKV = (NH + 2 * NKV) * HD
NT = S // P
KEYS = P + WINDOW
BLK = 64
NPAIR = NH // 2
KPAIR = NKV // 2
VW = 2 * HD
SLOT = 64
NE, TOPK, NGRP, TOPG, EPG = 16, 4, 4, 2, 4
ROUTED_SCALE = 2.5
F = 128
NF = NE + 2
CH = 512
NC = S // CH
TPC = CH // P
GU = KD * 2 * F
WCOLS = NF * GU + NF * D
WCH = WCOLS // NT
DOWN0 = NF * GU
NEG = -3.0e38
SCALE = HD ** -0.5
LN_EPS, RMS_EPS = 1e-5, 1e-6

C_ID, C_COS, C_SIN, C_TRI, C_NHALF = 0, P, P + NT * HD, P + 2 * NT * HD, P + 2 * NT * HD + 16
NCF = C_NHALF + 1
B_ID, B_MQ, B_MQ0, B_MT, B_MT0 = 0, P, P + KEYS, P + 2 * KEYS, P + 2 * KEYS + BLK
NCB = B_MT0 + BLK

BK_T, BK_PROJ, BK_S, BK_PV, BK_RING = 0, 1, 2, 3, 4
USES = "M0 M1 T0 T1 M2 T2 M3 T3 M4 M5 M6 M7 Q0 Q1 K2".split()
TR_USE = [USES.index(u) for u in ("Q0", "Q1", "K2")]
MAX_USE = [USES.index(f"M{i}") for i in range(NPAIR)]
T_USE = [USES.index(f"T{i}") for i in range(4)]


class Tile:

    def __init__(self, m, d):
        self.m, self.d, self.par = m, d, d % 2

    def __add__(self, k):
        return Tile(self.m, self.d + k)

    def times(self, per, extra=0):
        return self.m * (2 * per) + (per * self.d + extra)

    def half(self, per, extra=0):
        return self.m * per + (per * (self.d // 2) + extra)

    def static(self):
        return isinstance(self.m, int)

    def index(self):
        return self.times(1)


def bc(ap, at, n):
    dims = [list(x) for x in ap.ap]
    dims.insert(at, [0, n])
    return bass.AP(ap.tensor, ap.offset, dims)


def build(nc, x, wqkv, wo, rms_w, gate_weight, bias, wbig, c, wmod, cf, cb, out):
    x1_dram = nc.dram_tensor("x1_scratch", (S, D), F32, kind="Internal").ap()
    w_dram = nc.dram_tensor("expert_weights_scratch", (NE, S), F32, kind="Internal").ap()
    with ExitStack() as ctx:
        def sb(name, shape, dt=F32):
            return ctx.enter_context(nc.sbuf_tensor(name, shape, dt))

        def sem(name):
            return ctx.enter_context(nc.semaphore(name))

        banks = [ctx.enter_context(nc.psum_tensor(f"bank{i}", [P, 512], F32)) for i in range(8)]

        w_hi = sb("w_hi", [P, WCOLS], F32R)
        w_lo = sb("w_lo", [P, WCOLS], F32R)
        w_stage = sb("w_stage", [P, WCH])
        wqkv_s = sb("wqkv_s", [P, KD, QKV])
        wo_s = sb("wo_s", [P, KD, D])
        gw_s = sb("gw_s", [P, KD, NE])
        bias_s = sb("bias_s", [P, NE])
        rms_s = sb("rms_s", [P, KD])
        cf_s = sb("cf_s", [P, NCF])
        cb_s = sb("cb_s", [P, NCB], BF16)
        mod_rows = sb("mod_rows", [P, 2, D])
        mod_cols = sb("mod_cols", [P, 6])
        silu_c = sb("silu_c", [P, 4, KD])
        c_wide = sb("c_wide", [P, KD, P])
        h2_hi = sb("h2_hi", [P, KD, S], F32R)
        h2_lo = sb("h2_lo", [P, KD, S], F32R)
        xs = sb("xs", [P, 4, D])
        x1_o = sb("x1_o", [P, 2, D])
        scratch = sb("scratch", [P, 3072])
        qt = sb("qt", [P, 2, NPAIR, P], F32R)
        kt = sb("kt", [P, 2, KPAIR, KEYS], F32R)
        qs = sb("qs", [P, NH, SLOT])
        ks = sb("ks", [P, NKV, SLOT])
        xv = sb("xv", [P, S // 2])
        xnt = xv[:, 0:2 * KD * P].rearrange("p (s k t) -> p s k t", s=2, k=KD)
        vv = xv[:, 2 * KD * P:2 * KD * P + 4 * NKV * VW].rearrange("p (s w g d) -> p s w g d", s=2, w=2, g=NKV)
        rt = sb("rt", [P, 7, D])
        logits = sb("logits", [P, NT, NE])
        w_rows = xv[0:NE, :]
        stat = sb("stat", [P, 2, 6])
        mv = sb("mv", [P, 2, 2])
        tiny = sb("tiny", [P, 9])
        mx = sb("mx", [P, 2, NPAIR])
        ms = sb("ms", [P, 2, 2, NPAIR])
        cb_stage = rt[:, 0:3, :].rearrange("p a b -> p (a b)")[:, 0:NCB]
        rden = sb("rden", [P, NH])

        ident = cf_s[:, C_ID:C_ID + P]
        identb = cb_s[:, B_ID:B_ID + P]
        pt = [scratch[:, 512 * i:512 * i + 512] for i in range(2)]
        rope_a = scratch[:, 1024:1344]
        rope_b = scratch[:, 1344:1664]
        rope_o = scratch[:, 1664:1984]
        ot = scratch[:, 2304:2304 + 4 * P]
        mt = sb("mt", [4 * NPAIR, P], F32R)
        z, h, xn, attn, attnt, z2, h32 = (rt[:, i, :] for i in range(7))
        xa = [xs[:, 0, :], xs[:, 1, :]]
        xb = [xs[:, 2, :], xs[:, 3, :]]
        ve, rstd, ssq, msq, rrms, ve2, rstd2 = (tiny[:, i:i + 1] for i in range(7))
        nhalf = cf_s[:, C_NHALF:C_NHALF + 1]
        wmod_a = scratch[:, 2048:3072].rearrange("p (k n) -> p k n", k=KD)
        wmod_b = scratch[:, 0:2048].rearrange("p (k n) -> p k n", k=KD)

        s_const = sem("consts_loaded")
        s_wmod = sem("wmod_loaded")
        s_wmod2 = sem("wmod_rest_loaded")
        s_wqkv = sem("wqkv_loaded")
        s_small = sem("small_weights_loaded")
        s_su = sem("setup_step")
        s_su_act = sem("setup_exp")
        s_modp = sem("mod_product")
        s_ones = sem("fixed_parts_written")
        s_xa = [sem("xa_loaded0"), sem("xa_loaded1")]
        s_xb = [sem("xb_loaded0"), sem("xb_loaded1")]
        s_st = sem("ln1_stats")
        s_ag = sem("ln1_aggregated")
        s_ve = sem("ln1_variance")
        s_rstd = sem("ln1_rstd")
        s_z = sem("ln1_normal")
        s_hm = sem("h_scaled")
        s_h = sem("h_ready")
        s_ssq = sem("h_squares")
        s_msq = sem("h_mean_square")
        s_rrms = sem("h_rrms")
        s_xn = sem("xn_ready")
        s_xtr = sem("xn_transposed")
        s_xnt = sem("xnt_ready")
        s_proj = sem("projected")
        s_v = sem("v_ready")
        s_vw = [sem("v_shifted0"), sem("v_shifted1")]
        s_ra = sem("rope_products")
        s_ro = sem("rope_done")
        s_qkhi = sem("qk_high")
        s_qklo = sem("qk_low")
        s_qktr = sem("qk_transposed")
        s_qkt = sem("qkt_ready")
        s_sc = sem("scores_for_max")
        s_mxr = sem("max_read")
        s_ms = sem("max_parts")
        s_mtr = sem("max_transposed")
        s_mt = sem("max_rows_ready")
        s_md = sem("max_rows_placed")
        s_ts = sem("scores_transposed")
        s_ex = sem("probs_ready")
        s_pv = sem("weighted_values")
        s_ot = sem("sums_copied")
        s_on = sem("sums_transposed")
        s_rd = sem("denominator_inverted")
        s_at = sem("attn_ready")
        s_atr = sem("attn_transposed")
        s_att = sem("attnt_ready")
        s_wo = sem("attn_projected")
        s_x1 = sem("x1_ready")
        s_x1s = [sem("x1_stored0"), sem("x1_stored1")]
        s_st2 = sem("ln2_stats")
        s_ag2 = sem("ln2_aggregated")
        s_ve2 = sem("ln2_variance")
        s_rstd2 = sem("ln2_rstd")
        s_z2 = sem("z2_ready")
        s_z2tr = sem("z2_transposed")
        s_h32 = sem("h2_ready")
        s_h2hi = sem("h2_high")
        s_h2lo = sem("h2_low")
        s_lg = sem("logits_product")
        s_lgr = sem("logits_read")
        s_wl = sem("w_chunk_loaded")
        s_whi = sem("w_chunk_high")
        s_wlo = sem("w_chunk_low")

        s_r = sem("routing_step")
        s_rexp = sem("routing_exp")
        s_wtr = sem("weights_transposed")
        s_wt = sem("weights_row_ready")
        s_wst = sem("weights_stored")
        s_wbl = [sem("spread_weights_loaded0"), sem("spread_weights_loaded1")]
        s_g = sem("gate_product")
        s_u = sem("up_product")
        s_sl = sem("silu_ready")
        s_wsl = sem("weighted_silu_ready")
        s_a = sem("act_ready")
        s_ahi = sem("act_high")
        s_alo = sem("act_low")
        s_afree = sem("act_slot_free")
        s_yt = sem("ffn_scaled")
        s_ytr = sem("ffn_transposed")
        s_fin = sem("out_ready")
        s_x1l = sem("x1_chunk_loaded")
        s_out = [sem("out_stored0"), sem("out_stored1")]

        HT = NT // 2
        HW = HT * NE
        routing_steps = []
        r_bufs = rt[:, 0:3, :].rearrange("p a b -> p (a b)")
        gtmp = w_stage[:, 0:HT * 28]
        r_ex = [w_stage[:, HT * 28 + HW * i:HT * 28 + HW * (i + 1)] for i in range(2)]

        BK_G, BK_U, BK_Y, BK_YT = 4, 6, 0, 2
        BK_ROUTE = [(1, 3), (2, 3)]
        sl = [scratch[:, 0:512], scratch[:, 512:1024]]
        aa = [scratch[:, 1024:1536], scratch[:, 1536:2048]]
        wsl = scratch[:, 2048:2560]
        a_hi = [qt[:, 0, 4 * i:4 * i + 4, :].rearrange("p a b -> p (a b)") for i in range(2)]
        a_lo = [qt[:, 1, 4 * i:4 * i + 4, :].rearrange("p a b -> p (a b)") for i in range(2)]
        yt = qs[:].rearrange("p a b -> p (a b)").rearrange("p (k t) -> p k t", k=KD)

        w_all = [rt[:, 3 + 2 * i:5 + 2 * i, :].rearrange("p a b -> p (a b)") for i in range(2)]

        def ytok(pr):
            return x1_o[:, :, :] if pr == 0 else vtok

        vtok = scratch[:, 2560:3072].rearrange("p (t d) -> p t d", t=2)

        sq_junk = scratch[:, 2048:2304]
        ks2 = bass.AP(ks[:].tensor, ks[:].offset, [list(ks[:].ap[0]), [SLOT, NKV], [2 * HD, 2], [1, HD]]).bitcast(F32R)
        ROW_STEPS, COPY_STEPS, SETUP_STEPS = 6, 8, 18

        block = ctx.enter_context(nc.Block())

        LAST = 4

        def turns(eng, body):
            for j in range(LAST):
                body(Tile(0, j), j)
            with eng.Fori(LAST // 2, NT // 2) as m:
                for k in range(2):
                    body(Tile(m, k), None)
            for j in range(NT, NT + LAST):
                body(Tile(0, j), j)

        def live(j, lag):
            return j is None or 0 <= j - lag < NT

        def after(j, lag, back=1):
            return j is None or j - lag - back >= 0

        def shifted(t):
            return t.half(32, 16 if t.par == 0 else 32)

        def ring(u):
            return banks[BK_RING + u % 4]

        @block.sync
        def _(sp):
            sp.dma_start(cf_s[:], cf).then_inc(s_const, 16)
            sp.dma_start(cb_stage, cb).then_inc(s_const, 16)
            sp.dma_start(silu_c[:, 0, :], c).then_inc(s_const, 16)
            sp.dma_start(xa[0], x[0:P, :]).then_inc(s_xa[0], 16)
            for k in range(KD):
                sp.dma_start(wmod_a[:, k, :], wmod[P * k:P * (k + 1), 0:2 * D]).then_inc(s_wmod, 16)
            sp.dma_start(rms_s[:], rms_w).then_inc(s_wqkv, 16)
            sp.dma_start(wqkv_s[:], wqkv.rearrange("(k p) n -> p k n", p=P)).then_inc(s_wqkv, 16)
            for k in range(KD):
                sp.dma_start(wmod_b[:, k, :], wmod[P * k:P * (k + 1), 2 * D:6 * D]).then_inc(s_wmod2, 16)
            sp.dma_start(wo_s[:], wo.rearrange("(k p) n -> p k n", p=P)).then_inc(s_small, 16)
            sp.dma_start(gw_s[:], gate_weight.rearrange("(k p) n -> p k n", p=P)).then_inc(s_small, 16)
            sp.dma_start(bias_s[:], bc(bias.rearrange("(o n) -> o n", o=1)[0, :], 0, P)).then_inc(s_small, 16)

            def body(t, j):
                if live(j, 0) and j != 0:
                    if after(j, 0, 2):
                        sp.wait_ge(s_z, t.times(1, -1))
                    sp.dma_start(xa[t.par], x[bass.ds(t.times(P), P), :]).then_inc(s_xa[t.par], 16)
                n = t + (-3)
                if live(j, 3):
                    sp.wait_ge(s_mt, n.times(1, 1))
                    for hf in range(2):
                        for part in range(2):
                            r = (2 * hf + part) * NPAIR
                            row = 64 * hf + 3 * HD + part
                            sp.dma_start(qt[row:row + 1, n.par, :, :].bitcast(F32), mt[r:r + NPAIR, :].bitcast(F32)).then_inc(s_md, 16)
                n = t + (-2)
                if live(j, 2):
                    sp.wait_ge(s_v, n.times(1, 1))
                    if after(j, 2):
                        sp.dma_start(vv[0:WINDOW, n.par, 1, :, :], vv[WINDOW:P, 1 - n.par, 0, :, :]).then_inc(s_vw[n.par], 16)
                    sp.dma_start(vv[WINDOW:P, n.par, 1, :, :], vv[0:P - WINDOW, n.par, 0, :, :]).then_inc(s_vw[n.par], 16)
                n = t + (-4)
                if live(j, 4):
                    sp.wait_ge(s_x1, n.times(1, 1))
                    sp.dma_start(x1_dram[bass.ds(n.times(P), P), :], x1_o[:, n.par, :]).then_inc(s_x1s[n.par], 16)
                n = t + (-2)
                if live(j, 2):
                    if after(j, 2, 2):
                        sp.wait_ge(s_x1, n.times(1, -1))
                    sp.dma_start(xb[n.par], x[bass.ds(n.times(P), P), :]).then_inc(s_xb[n.par], 16)
                if live(j, 0):
                    if after(j, 0):
                        sp.wait_ge(s_wlo, t.times(1))
                    sp.dma_start(w_stage[:], wbig[bass.ds(t.index(), 1), :, :].rearrange("o p n -> (o p) n")).then_inc(s_wl, 16)

            turns(sp, body)
            for par in range(2):
                sp.wait_ge(s_x1s[par], 16 * NT // 2)
            for pr in range(2):
                sp.sem_inc(s_out[pr], 16)

            def x1_load(ci):
                sp.wait_ge(s_fin, ci * 2 + 2)
                sp.dma_start(xs[:], x1_dram[bass.ds(ci * CH, CH), :].rearrange("(t p) d -> p t d", p=P)).then_inc(s_x1l, 16)

            def store_weights(half):
                sp.wait_ge(s_wt, 2 * half + 2)
                sp.dma_start(w_dram[:, S // 2 * half:S // 2 * (half + 1)], w_rows).then_inc(s_wst, 16)
                sp.wait_ge(s_wst, 16 * (half + 1))

            def spread(ci, i):
                cn, k = ci + i // NF, i % NF + (2 if i >= NF else 0)
                if not (isinstance(cn, int) and cn == 0 and k < 4):
                    sp.wait_ge(s_wsl, cn * NE + (k - 2))
                sp.dma_start(w_all[k % 2], bc(w_dram[k - 2, bass.ds(cn * CH, CH)], 0, P)).then_inc(s_wbl[k % 2], 16)

            def chunk(ci, last, second_half):
                for i in range(4, NF):
                    spread(ci, i)
                    if second_half and i == 15:
                        store_weights(1)
                if not last:
                    spread(ci, NF)
                    spread(ci, NF + 1)
                for pr in range(2):
                    sp.wait_ge(s_fin, ci * 2 + (pr + 3))
                    sp.dma_start(out[bass.ds(ci * CH + 2 * P * pr, 2 * P), :].rearrange("(t p) d -> p t d", p=P),
                                 ytok(pr)).then_inc(s_out[pr], 16)
                if not last:
                    x1_load(ci + 1)

            x1_load(0)
            store_weights(0)
            sp.wait_ge(s_wo, NT)
            spread(0, 2)
            sp.wait_ge(s_lg, NT)
            sp.wait_ge(s_h2lo, NT)
            spread(0, 3)
            chunk(0, False, True)
            with sp.Fori(1, NC - 1) as ci:
                chunk(ci, False, False)
            chunk(NC - 1, True, False)
            for pr in range(2):
                sp.wait_ge(s_out[pr], 16 * NC + 16)

        @block.gpsimd
        def _(pool):
            g = nc.gpsimd
            pool.wait_ge(s_const, 48)

            def body(t, j):
                if live(j, 0):
                    pool.wait_ge(s_ve, t.times(1, 1))
                    g.tensor_tensor(rstd, ve, nhalf, ALU.pow).then_inc(s_rstd, 1)
                n = t + (-1)
                if live(j, 1):
                    pool.wait_ge(s_whi, n.times(1, 1))
                    pool.wait_ge(s_const, 48)
                    at = n.times(WCH)
                    g.tensor_tensor(w_lo[:, bass.ds(at, WCH)], w_stage[:], w_hi[:, bass.ds(at, WCH)].bitcast(F32), ALU.subtract).then_inc(s_wlo, 1)
                n = t + (-4)
                if live(j, 4):
                    pool.wait_ge(s_ve2, n.times(1, 1))
                    g.tensor_tensor(rstd2, ve2, nhalf, ALU.pow).then_inc(s_rstd2, 1)
                if live(j, 0):
                    pool.wait_ge(s_z, t.times(1, 1))
                    if j == 0:
                        pool.wait_ge(s_su, ROW_STEPS)
                    if after(j, 0):
                        pool.wait_ge(s_xn, t.times(1))
                    g.tensor_tensor(h, z, mod_rows[:, 1, :], ALU.mult).then_inc(s_hm, 1)
                    pool.wait_ge(s_hm, t.times(1, 1))
                    g.tensor_tensor(h, h, mod_rows[:, 0, :], ALU.add).then_inc(s_h, 1)
                n = t + (-1)
                if live(j, 1):
                    pool.wait_ge(s_qkhi, n.times(2, 2))
                    o = rope_o.rearrange("p (n d) -> p n d", d=HD)
                    if after(j, 1):
                        pool.wait_ge(s_qktr, n.times(3))
                    g.tensor_tensor(qs[:, :, 2 * HD:3 * HD].bitcast(F32R), o[:, 0:NH, :], qs[:, :, 0:HD], ALU.subtract).then_inc(s_qklo, 1)
                    g.tensor_tensor(ks[:, :, HD:2 * HD].bitcast(F32R), o[:, NH:NQK, :], ks[:, :, 0:HD], ALU.subtract).then_inc(s_qklo, 1)
                if live(j, 0):
                    pool.wait_ge(s_msq, t.times(1, 1))
                    g.tensor_tensor(rrms, msq, nhalf, ALU.pow).then_inc(s_rrms, 1)
                n = t + (-4)
                if live(j, 4):
                    pool.wait_ge(s_h2hi, n.times(1, 1))
                    at = bass.ds(n.times(P), P)
                    g.tensor_tensor(h2_lo[:, :, at], h32.rearrange("p (k t) -> p k t", k=KD), h2_hi[:, :, at].bitcast(F32),
                                    ALU.subtract).then_inc(s_h2lo, 1)

            turns(pool, body)

        @block.vector
        def _(dve):
            v = nc.vector
            step = [0]
            dve.sem_inc(s_a, 2)
            dve.sem_inc(s_wsl, 1)
            dve.sem_inc(s_fin, 2)

            def chain(ins, sem_=s_su):
                step[0] += 1
                ins.then_inc(sem_, 1)
                dve.wait_ge(sem_, step[0])

            v.memset(qs[:], 0.0).then_inc(s_ones, 1)
            v.memset(ks[:], 0.0).then_inc(s_ones, 1)
            v.memset(kt[:, 0, :, 0:WINDOW].bitcast(F32), 0.0).then_inc(s_ones, 1)
            v.memset(vv, 1.0).then_inc(s_ones, 1)
            dve.wait_ge(s_ones, 4)
            v.memset(ks[:, :, 3 * HD:3 * HD + 2], -1.0).then_inc(s_ones, 1)

            dve.wait_ge(s_const, 48)
            v.tensor_copy(cb_s[:], cb_stage).then_inc(s_ones, 1)
            dve.wait_ge(s_su_act, 1)
            chain(v.tensor_scalar(silu_c[:, 2, :], silu_c[:, 1, :], 1.0, None, ALU.add))
            chain(v.reciprocal(silu_c[:, 3, :], silu_c[:, 2, :]))
            chain(v.tensor_tensor(silu_c[:, 1, :], silu_c[:, 0, :], silu_c[:, 3, :], ALU.mult))
            chain(v.tensor_copy(c_wide[:], bc(silu_c[:, 1, :], 2, P)))
            dve.wait_ge(s_wqkv, 32)
            for k in range(KD):
                v.tensor_scalar(wqkv_s[:, k, :], wqkv_s[:, k, :], rms_s[:, k:k + 1], None, ALU.mult).then_inc(s_ones, 1)

            def setup_rows():
                dve.wait_ge(s_modp, 1)
                chain(v.tensor_copy(mod_rows[:, 0, :], banks[4][:, 0:D]))
                chain(v.tensor_scalar(mod_rows[:, 1, :], banks[4][:, D:2 * D], 1.0, None, ALU.add))
                assert step[0] == ROW_STEPS, step[0]

            def gate(g, mag, sgn, to):
                chain(v.scalar_tensor_tensor(mag, g, -1.0, g, ALU.mult, ALU.max))
                chain(v.tensor_scalar(mag, mag, 0.25, None, ALU.max))
                chain(v.tensor_scalar(sgn, g, 0.0, 2.0, ALU.is_ge, ALU.mult))
                return v.scalar_tensor_tensor(to, sgn, -1.0, mag, ALU.add, ALU.mult)

            def setup_copies():
                dve.wait_ge(s_modp, 2)
                chain(v.tensor_copy(mod_cols[:], banks[6][:, 0:6]))
                chain(v.tensor_copy(z2, banks[5][:, 0:D]))
                assert step[0] == COPY_STEPS, step[0]

            def setup_rest():
                chain(v.tensor_scalar(mod_cols[:, 2:4], mod_cols[:, 2:4], 1.0, None, ALU.add))
                chain(gate(z2, attn, attnt, z2))
                chain(gate(mod_cols[:, 4:6], rden[:, 0:2], rden[:, 2:4], mod_cols[:, 4:6]))
                dve.wait_ge(s_small, 48)
                chain(v.tensor_tensor(wo_s[:], wo_s[:], bc(z2, 1, KD), ALU.mult))
                assert step[0] == SETUP_STEPS, step[0]
                step[0] = 0

            def maxima(t, parts):
                for q in parts:
                    a, hf = q // 2, q % 2
                    dve.wait_ge(s_sc, t.times(8, q + 1))
                    v.tensor_reduce(mx[:, hf, 2 * a:2 * a + 2],
                                    ring(MAX_USE[q])[:, 0:2 * KEYS].rearrange("p (h k) -> p h k", h=2),
                                    AX.X, ALU.max).then_inc(s_mxr, 1)

            E3 = lambda a: a.rearrange("p (t e) -> p t e", e=NE)
            G4 = lambda a: a.rearrange("p (t g e) -> p t g e", g=NGRP, e=EPG)
            sc, ch, mk, rep, wgt, tmp = (r_bufs[:, HW * i:HW * (i + 1)] for i in range(6))

            def link(ins):
                chain(ins, s_r)

            def route_scores(half):
                dve.wait_ge(s_rexp, half + 1)
                if half == 0:
                    dve.wait_ge(s_wlo, NT)
                link(v.tensor_scalar(tmp, r_ex[half], 1.0, None, ALU.add))
                link(v.reciprocal(sc, tmp))
                link(v.tensor_tensor(E3(ch), E3(sc), bc(bias_s[:], 1, HT), ALU.add))
                c4 = G4(ch)
                prs = gtmp[:, 0:HT * 24].rearrange("p (t g s) -> p t g s", g=NGRP, s=6)
                v.tensor_tensor(prs[:, :, :, 0:3], c4[:, :, :, 0:3], c4[:, :, :, 1:4], ALU.add)
                v.tensor_tensor(prs[:, :, :, 3:5], c4[:, :, :, 0:2], c4[:, :, :, 2:4], ALU.add)
                link(v.tensor_tensor(prs[:, :, :, 5:6], c4[:, :, :, 0:1], c4[:, :, :, 3:4], ALU.add))
                link(v.tensor_reduce(gtmp[:, HT * 24:HT * 28].rearrange("p (t g) -> p t g", g=NGRP), prs, AX.X, ALU.max))

            def route_groups(half):
                gs = gtmp[:, HT * 24:HT * 28].rearrange("p (t g) -> p t g", g=NGRP)
                ex = r_ex[half]
                other, own = bc(gs, 2, NGRP), bc(gs, 3, NGRP)
                tri = bc(cf_s[:, C_TRI:C_TRI + 16].rearrange("p (a b) -> p a b", b=NGRP), 1, HT)
                v.tensor_tensor(G4(tmp), other, own, ALU.is_gt)
                link(v.tensor_tensor(G4(ex), other, own, ALU.is_equal))
                link(v.tensor_tensor(G4(ex), G4(ex), tri, ALU.mult))
                link(v.tensor_tensor(tmp, tmp, ex, ALU.add))
                rank = gtmp[:, 0:HT * NGRP].rearrange("p (t g) -> p t g", g=NGRP)
                link(v.tensor_reduce(rank, G4(tmp), AX.X, ALU.add))
                gm = gtmp[:, HT * NGRP:2 * HT * NGRP].rearrange("p (t g) -> p t g", g=NGRP)
                gn = gtmp[:, 2 * HT * NGRP:3 * HT * NGRP].rearrange("p (t g) -> p t g", g=NGRP)
                v.tensor_scalar(gm, rank, TOPG - 0.5, None, ALU.is_lt)
                link(v.tensor_scalar(gn, rank, TOPG - 0.5, NEG, ALU.is_gt, ALU.mult))
                link(v.tensor_tensor(G4(mk), G4(ch), bc(gm, 3, EPG), ALU.mult))
                link(v.tensor_tensor(G4(mk), G4(mk), bc(gn, 3, EPG), ALU.add))

            def route_top():
                top = gtmp[:, 0:HT * 8].rearrange("p (t k) -> p t k", k=8)
                for i in range(HT):
                    ins = v.max(top[:, i, :], E3(mk)[:, i, :])
                link(ins)
                link(v.memset(top[:, :, TOPK:8], 2.0e38))
                for i in range(HT):
                    ins = v.match_replace(E3(rep)[:, i, :], top[:, i, :], E3(mk)[:, i, :], -NEG)
                link(ins)
                link(v.tensor_scalar(rep, rep, 1.0e38, None, ALU.is_gt))

            def route_weights(half):
                link(v.tensor_tensor(wgt, sc, rep, ALU.mult))
                sm = gtmp[:, 0:HT]
                link(v.tensor_reduce(sm, E3(wgt), AX.X, ALU.add))
                link(v.tensor_scalar(sm, sm, 1e-20, None, ALU.add))
                link(v.reciprocal(gtmp[:, HT:2 * HT], sm))
                link(v.tensor_tensor(E3(wgt), E3(wgt), bc(gtmp[:, HT:2 * HT], 2, NE), ALU.mult))
                link(v.tensor_scalar(wgt, wgt, ROUTED_SCALE, None, ALU.mult))
                routing_steps.append(step[0])

            def route_rows(half):
                dve.wait_ge(s_wtr, half + 1)
                if half:
                    dve.wait_ge(s_wst, 16)
                for q in range(2):
                    v.tensor_copy(w_rows[:, 4 * P * q:4 * P * (q + 1)], banks[BK_ROUTE[half][q]][0:NE, :]).then_inc(s_wt, 1)

            def act_(ci, i):
                nn = ci * NF + i
                dve.wait_ge(s_u, nn + 1)
                left = sl[i % 2] if i % NF < 2 else wsl
                if i % NF < 2:
                    dve.wait_ge(s_sl, nn + 3)
                else:
                    dve.wait_ge(s_wsl, ci * NE + i)
                v.tensor_tensor(aa[i % 2], left, banks[BK_U + i % 2][:], ALU.mult).then_inc(s_a, 1)

            def low(ci, i):
                nn = ci * NF + i
                dve.wait_ge(s_ahi, nn + 1)
                v.tensor_tensor(a_lo[i % 2], aa[i % 2], a_hi[i % 2].bitcast(F32), ALU.subtract).then_inc(s_alo, 1)

            def weighted(ci, i):
                nn = ci * NF + i
                dve.wait_ge(s_sl, nn + 3)
                dve.wait_ge(s_wbl[i % 2], ci * 128 + 16 * (i // 2))
                v.tensor_tensor(wsl, sl[i % 2], w_all[i % 2], ALU.mult).then_inc(s_wsl, 1)

            def body(t, j):
                c_ = t + (-2)
                if live(j, 0):
                    dve.wait_ge(s_xa[t.par], t.half(16, 16))
                    v.bn_stats(stat[:, 0, :], xa[t.par]).then_inc(s_st, 1)
                if live(j, 2):
                    if after(j, 2):
                        dve.wait_ge(s_ms, c_.times(2))
                    maxima(c_, range(1))
                if live(j, 0):
                    dve.wait_ge(s_st, t.times(1, 1))
                    v.tensor_copy(tiny[:, 8:9], stat[:, 0, 0:1])
                    v.bn_aggr(mv[:, 0, :], stat[:, 0, :]).then_inc(s_ag, 1)
                if live(j, 2):
                    maxima(c_, range(1, 2))
                if live(j, 0):
                    dve.wait_ge(s_ag, t.times(1, 1))
                    v.tensor_scalar(ve, mv[:, 0, 1:2], LN_EPS, None, ALU.add).then_inc(s_ve, 1)
                n = t + (-4)
                if live(j, 4):
                    dve.wait_ge(s_wo, n.times(1, 1))
                    dve.wait_ge(s_xb[n.par], n.half(16, 16))
                    if after(j, 4, 2):
                        dve.wait_ge(s_x1s[n.par], n.half(16))
                    v.tensor_tensor(x1_o[:, n.par, :], banks[BK_PV][:, 0:D], xb[n.par], ALU.add).then_inc(s_x1, 1)
                    dve.wait_ge(s_x1, n.times(1, 1))
                    v.bn_stats(stat[:, 1, :], x1_o[:, n.par, :]).then_inc(s_st2, 1)
                    dve.wait_ge(s_st2, n.times(1, 1))
                    v.tensor_copy(tiny[:, 7:8], stat[:, 1, 0:1])
                    v.bn_aggr(mv[:, 1, :], stat[:, 1, :]).then_inc(s_ag2, 1)
                    dve.wait_ge(s_ag2, n.times(1, 1))
                    v.tensor_scalar(ve2, mv[:, 1, 1:2], LN_EPS, None, ALU.add).then_inc(s_ve2, 1)
                if live(j, 0):
                    dve.wait_ge(s_rstd, t.times(1, 1))
                    if after(j, 0):
                        dve.wait_ge(s_h, t.times(1))
                    v.tensor_scalar(z, xa[t.par], mv[:, 0, 0:1], rstd, ALU.subtract, ALU.mult).then_inc(s_z, 1)
                if j == 0:
                    setup_rows()
                n = t + (-1)
                if live(j, 1):
                    dve.wait_ge(s_proj, n.times(1, 1))
                    src = banks[BK_PROJ][:, 0:NQK * HD].rearrange("p (n d) -> p n d", d=HD)
                    sw = bass.AP(src.tensor, src.offset + 1, [list(src.ap[0]), [HD, NQK], [2, HD // 2], [-1, 2]])
                    cos = bc(cf_s[:, bass.ds(n.times(HD, C_COS), HD)], 1, NQK)
                    sin = bc(cf_s[:, bass.ds(n.times(HD, C_SIN), HD)].rearrange("p (i j) -> p i j", j=2), 1, NQK)
                    v.tensor_tensor(rope_a.rearrange("p (n d) -> p n d", d=HD), src, cos, ALU.mult).then_inc(s_ra, 1)
                    v.tensor_tensor(rope_b.rearrange("p (n i j) -> p n i j", i=HD // 2, j=2), sw, sin, ALU.mult).then_inc(s_ra, 1)
                    dve.wait_ge(s_ra, n.times(2, 2))
                    if after(j, 1):
                        dve.wait_ge(s_qklo, n.times(2))
                    v.tensor_tensor(rope_o, rope_a, rope_b, ALU.add).then_inc(s_ro, 1)
                n = t + (-4)
                if live(j, 4):
                    dve.wait_ge(s_rstd2, n.times(1, 1))
                    if after(j, 4):
                        dve.wait_ge(s_z2tr, n.times(1))
                    v.tensor_scalar(z2, x1_o[:, n.par, :], mv[:, 1, 0:1], rstd2, ALU.subtract, ALU.mult).then_inc(s_z2, 1)
                if j == NT + 2:
                    route_groups(0)
                if j == NT + 3:
                    route_weights(0)
                if live(j, 2):
                    maxima(c_, range(2, 6))
                if live(j, 0):
                    dve.wait_ge(s_ssq, t.times(1, 1))
                    v.tensor_scalar(msq, ssq, 1.0 / D, RMS_EPS, ALU.mult, ALU.add).then_inc(s_msq, 1)
                if live(j, 2):
                    maxima(c_, range(6, 8))
                    dve.wait_ge(s_mxr, c_.times(8, 8))
                    if after(j, 2):
                        dve.wait_ge(s_mtr, c_.times(1))
                    v.tensor_copy(ms[:, :, 0, :].bitcast(F32R), mx[:]).then_inc(s_ms, 1)
                    dve.wait_ge(s_ms, c_.times(2, 1))
                    v.tensor_tensor(ms[:, :, 1, :].bitcast(F32R), mx[:], ms[:, :, 0, :], ALU.subtract).then_inc(s_ms, 1)
                d_ = t + (-3)
                if j == 1:
                    setup_copies()
                if live(j, 3):
                    pv = banks[BK_PV][:].rearrange("p (h d) -> p h d", h=NH)
                    dve.wait_ge(s_on, d_.times(1, 1))
                    v.reciprocal(rden[:], pv[:, :, HD]).then_inc(s_rd, 1)
                    dve.wait_ge(s_rd, d_.times(1, 1))
                    if after(j, 3):
                        dve.wait_ge(s_atr, d_.times(1))
                    v.tensor_tensor(attn.rearrange("p (h d) -> p h d", h=NH), pv[:, :, 0:HD],
                                    bc(rden[:], 2, HD), ALU.mult).then_inc(s_at, 1)
                if j == NT + 2:
                    route_top()
                if live(j, 0):
                    dve.wait_ge(s_rrms, t.times(1, 1))
                    if after(j, 0):
                        dve.wait_ge(s_xtr, t.times(1))
                    v.tensor_scalar(xn, h, rrms, None, ALU.mult).then_inc(s_xn, 1)
                if j == 1:
                    setup_rest()
                if live(j, 4):
                    dve.wait_ge(s_lg, n.times(1, 1))
                    v.tensor_scalar(logits[:, bass.ds(n.index(), 1), :].rearrange("p o e -> p (o e)"),
                                    banks[BK_S][:, 0:NE], 1.0, None, ALU.mult).then_inc(s_lgr, 1)
                if j == NT + 1:
                    route_scores(0)

            turns(dve, body)

            route_rows(0)
            act_(0, 0)
            low(0, 0)
            act_(0, 1)
            low(0, 1)

            def chunk(ci, last, second_half):
                weighted(ci, 2)
                for i in range(2, NF):
                    act_(ci, i)
                    low(ci, i)
                    if i + 1 < NF:
                        weighted(ci, i + 1)
                    if second_half and i == 4:
                        route_scores(1)
                    if second_half and i == 6:
                        route_groups(1)
                    if second_half and i == 8:
                        route_top()
                    if second_half and i == 10:
                        route_weights(1)
                    if second_half and i == 12:
                        route_rows(1)
                if not last:
                    act_(ci, NF)
                    low(ci, NF)
                for pr in range(2):
                    dve.wait_ge(s_ytr, ci * 2 + (pr + 1))
                    if pr == 0:
                        dve.wait_ge(s_x1l, ci * 16 + 16)
                    dve.wait_ge(s_out[pr], ci * 16 + 16)
                    v.tensor_tensor(ytok(pr), banks[BK_YT + pr][:].rearrange("p (t d) -> p t d", t=2),
                                    xs[:, 2 * pr:2 * pr + 2, :], ALU.add).then_inc(s_fin, 1)
                if not last:
                    act_(ci, NF + 1)
                    low(ci, NF + 1)

            chunk(0, False, True)
            with dve.Fori(1, NC - 1) as ci:
                chunk(ci, False, False)
            chunk(NC - 1, True, False)

        @block.scalar
        def _(act):
            a = nc.scalar
            act.sem_inc(s_sl, 2)
            act.sem_inc(s_yt, 2)
            act.wait_ge(s_const, 48)
            a.activation(silu_c[:, 1, :], silu_c[:, 0, :], ACT.Exp, scale=-1.0).then_inc(s_su_act, 1)

            def exps(n, j, i):
                u = T_USE[i]
                act.wait_ge(s_ts, n.times(4, i + 1))
                if i >= 2 or after(j, 3):
                    act.wait_ge(s_pv, n.times(4, i - 1))
                a.activation(pt[i % 2], ring(u)[:], ACT.Exp, scale=SCALE).then_inc(s_ex, 1)

            def evac(n, j, i):
                act.wait_ge(s_qktr, n.times(3, i + 1))
                b = ring(TR_USE[i])[:, 0:P * (4 if i < 2 else KPAIR)].rearrange("p (a t) -> p a t", t=P)
                if i == 0 and after(j, 1, 2):
                    act.wait_ge(s_ts, n.times(4, -4))
                if i < 2:
                    a.activation(qt[:, n.par, 4 * i:4 * i + 4, :], b, ACT.Copy).then_inc(s_qkt, 1)
                else:
                    if after(j, 1):
                        act.wait_ge(s_qkt, n.times(4))
                        a.activation(kt[:, n.par, :, 0:WINDOW], kt[:, 1 - n.par, :, P:KEYS].bitcast(F32), ACT.Copy).then_inc(s_qkt, 1)
                    a.activation(kt[:, n.par, :, WINDOW:KEYS], b, ACT.Copy).then_inc(s_qkt, 1 if after(j, 1) else 2)

            def body(t, j):
                n = t + (-1)
                if live(j, 1):
                    act.wait_ge(s_xtr, n.times(1, 1))
                    if after(j, 1, 2):
                        act.wait_ge(s_proj, n.times(1, -1))
                    a.activation(xnt[:, n.par, :, :], banks[BK_T][:, 0:D].rearrange("p (k t) -> p k t", k=KD),
                                 ACT.Copy).then_inc(s_xnt, 1)
                    act.wait_ge(s_wl, n.times(16, 16))
                    act.wait_ge(s_const, 48)
                    a.activation(w_hi[:, bass.ds(n.times(WCH), WCH)], w_stage[:], ACT.Copy).then_inc(s_whi, 1)
                m = t + (-3)
                if live(j, 3):
                    for i in range(2):
                        exps(m, j, i)
                if live(j, 1):
                    act.wait_ge(s_ro, n.times(1, 1))
                    if after(j, 1):
                        act.wait_ge(s_qktr, n.times(3))
                    o = rope_o.rearrange("p (n d) -> p n d", d=HD)
                    a.activation(qs[:, :, 0:2 * HD].rearrange("p h (r d) -> p h r d", r=2).bitcast(F32R),
                                 bc(o[:, 0:NH, :], 2, 2), ACT.Copy).then_inc(s_qkhi, 1)
                    a.activation(ks2, bc(o[:, NH:NQK, :], 2, 2), ACT.Copy).then_inc(s_qkhi, 1)
                if live(j, 3):
                    exps(m, j, 2)
                if live(j, 0):
                    act.wait_ge(s_h, t.times(1, 1))
                    if after(j, 0):
                        act.wait_ge(s_msq, t.times(1))
                    a.activation(sq_junk, h, ACT.Square, accum_out=ssq).then_inc(s_ssq, 1)
                if live(j, 3):
                    exps(m, j, 3)
                f_ = t + (-4)
                if live(j, 4):
                    act.wait_ge(s_z2tr, f_.times(1, 1))
                    if after(j, 4):
                        act.wait_ge(s_lg, f_.times(1))
                        act.wait_ge(s_h2lo, f_.times(1))
                    for k in range(KD):
                        a.activation(h32[:, P * k:P * (k + 1)], banks[BK_T][:, P * k:P * (k + 1)], ACT.Identity,
                                     bias=mod_cols[:, k:k + 1], scale=mod_cols[:, 2 + k:3 + k]).then_inc(s_h32, 1)
                    act.wait_ge(s_h32, f_.times(2, 2))
                    a.activation(h2_hi[:, :, bass.ds(f_.times(P), P)], h32.rearrange("p (k t) -> p k t", k=KD),
                                 ACT.Copy).then_inc(s_h2hi, 1)
                if live(j, 3):
                    act.wait_ge(s_pv, m.times(4, 4))
                    if after(j, 3):
                        act.wait_ge(s_on, m.times(1))
                    a.activation(ot, banks[BK_PV][:], ACT.Copy).then_inc(s_ot, 1)
                n = t + (-1)
                if live(j, 1):
                    act.wait_ge(s_ra, n.times(2, 2))
                    if j == 1:
                        act.wait_ge(s_ones, 8)
                    if after(j, 1, 2):
                        act.wait_ge(s_pv, n.times(4, -4))
                        act.wait_ge(s_vw[1 - n.par], shifted(n + (-1)))
                    a.activation(vv[:, n.par, 0, :, 0:HD],
                                 banks[BK_PROJ][:, NQK * HD:QKV].rearrange("p (g d) -> p g d", g=NKV),
                                 ACT.Copy).then_inc(s_v, 1)
                if live(j, 1):
                    evac(n, j, 0)
                n = t + (-2)
                if live(j, 2):
                    act.wait_ge(s_mtr, n.times(1, 1))
                    if after(j, 2):
                        act.wait_ge(s_md, n.times(64))
                    a.activation(mt[:], banks[BK_S][0:4 * NPAIR, 0:P], ACT.Copy).then_inc(s_mt, 1)
                n = t + (-1)
                if live(j, 1):
                    evac(n, j, 1)
                    evac(n, j, 2)
                if live(j, 3):
                    act.wait_ge(s_atr, m.times(1, 1))
                    if after(j, 3):
                        act.wait_ge(s_wo, m.times(1))
                    a.activation(attnt, banks[BK_PROJ][:, 0:D], ACT.Copy).then_inc(s_att, 1)
                if j == NT:
                    act.wait_ge(s_lgr, HT)
                    act.wait_ge(s_wlo, NT)
                    a.activation(r_ex[0], logits[:, 0:HT, :].rearrange("p t e -> p (t e)"), ACT.Exp, scale=-1.0).then_inc(s_rexp, 1)

            turns(act, body)

            def silu(ci, i):
                nn = ci * NF + i
                act.wait_ge(s_g, nn + 1)
                act.wait_ge(s_a, nn + 1)
                a.activation(sl[i % 2], banks[BK_G + i % 2][:], ACT.Silu).then_inc(s_sl, 1)

            def high(ci, i):
                nn = ci * NF + i
                act.wait_ge(s_a, nn + 3)
                act.wait_ge(s_afree, nn + 1)
                a.activation(a_hi[i % 2], aa[i % 2], ACT.Copy).then_inc(s_ahi, 1)

            def chunk(ci, last):
                for i in range(2, NF):
                    if i + 1 < NF or not last:
                        silu(ci, i + 1)
                    high(ci, i)
                if not last:
                    high(ci, NF)
                    silu(ci, NF + 1)
                for k in range(KD):
                    act.wait_ge(s_afree, ci * NF + (NF + 2))
                    a.activation(yt[:, k, :], banks[BK_Y + k][:], ACT.Copy, scale=mod_cols[:, 4 + k:5 + k]).then_inc(s_yt, 1)
                if not last:
                    silu(ci, NF + 2)
                    high(ci, NF + 1)

            silu(0, 0)
            act.wait_ge(s_lgr, NT)
            a.activation(r_ex[1], logits[:, HT:NT, :].rearrange("p t e -> p (t e)"), ACT.Exp, scale=-1.0).then_inc(s_rexp, 1)
            high(0, 0)
            silu(0, 1)
            high(0, 1)
            silu(0, 2)
            with act.Fori(0, NC - 1) as ci:
                chunk(ci, False)
            chunk(NC - 1, True)

        @block.tensor
        def _(pe):
            mm = nc.tensor.matmul
            tr = nc.tensor.transpose

            pe.wait_ge(s_su, 4)
            pe.wait_ge(s_wmod, 16 * KD)
            for k in range(KD):
                last = mm(banks[4][:, 0:2 * D], c_wide[:, k, :], wmod_a[:, k, :], start=(k == 0), stop=(k == KD - 1))
            last.then_inc(s_modp, 1)
            pe.wait_ge(s_wmod2, 16 * KD)
            for k in range(KD):
                mm(banks[5][:, 0:D], c_wide[:, k, :], wmod_b[:, k, 0:D], start=(k == 0), stop=(k == KD - 1))
            for i in range(6):
                for k in range(KD):
                    last = mm(banks[6][:, i:i + 1], wmod_b[:, k, D + P * i:D + P * (i + 1)], silu_c[:, 1, k:k + 1],
                              start=(k == 0), stop=(k == KD - 1))
            last.then_inc(s_modp, 1)
            pe.wait_ge(s_ones, 8)
            pe.wait_ge(s_const, 48)

            def free(t, j, use):
                u = USES.index(use)
                same = u >= 4
                last = USES[u - 4] if same else USES[u + 12 if u < 3 else 11]
                i = int(last[1])
                if last[0] == "M" and live(j if same or j is None else j - 1, 2):
                    c_ = t + (-2 if same else -3)
                    pe.wait_ge(s_mxr, c_.times(8, i + 1))
                elif last[0] == "T" and live(j, 3):
                    pe.wait_ge(s_ex, (t + (-3)).times(4, i + 1))
                elif last[0] in "QK" and live(j, 2):
                    pe.wait_ge(s_qkt, (t + (-2)).times(4, i + 1 if i < 2 else 4))

            def maxpass(t, j, parts):
                n = t + (-2)
                for q in parts:
                    a_, hf, b = q // 2, q % 2, ring(MAX_USE[q])
                    free(t, j, f"M{q}")
                    mq = B_MQ0 if j == 2 else B_MQ
                    if q == 0:
                        pe.wait_ge(s_qkt, n.times(4, 4))
                    mm(b[:, 0:2 * KEYS], identb, bc(cb_s[:, mq:mq + KEYS], 1, 2), start=True, stop=True)
                    for i in range(2):
                        p_ = 2 * a_ + i
                        last = mm(b[:, i * KEYS:(i + 1) * KEYS], qt[64 * hf:64 * hf + 3 * HD, n.par, p_, :],
                                  kt[64 * hf:64 * hf + 3 * HD, n.par, p_ // 4, :], start=False, stop=True, skip_group_check=True)
                    last.then_inc(s_sc, 1)

            def tpass(t, j, i):
                n = t + (-3)
                b2, hf, b = i // 2, i % 2, ring(T_USE[i])
                free(t, j, f"T{i}")
                mq = B_MT0 if j == 3 and b2 == 0 else B_MT
                if i == 0:
                    pe.wait_ge(s_md, n.times(64, 64))
                mm(b[:], identb, bc(cb_s[:, mq:mq + BLK], 1, NPAIR), start=True, stop=True)
                R = 3 * HD + 2
                for a_ in range(KPAIR):
                    last = mm(b[:, 2 * P * a_:2 * P * (a_ + 1)], kt[64 * hf:64 * hf + R, n.par, a_, BLK * b2:BLK * b2 + P],
                              qt[64 * hf:64 * hf + R, n.par, 4 * a_:4 * a_ + 4, BLK * b2:BLK * (b2 + 1)],
                              start=False, stop=True, skip_group_check=True)
                last.then_inc(s_ts, 1)

            def values(n, i):
                b2, hf = i // 2, i % 2
                pe.wait_ge(s_ex, n.times(4, i + 1))
                if i == 0:
                    pe.wait_ge(s_v, n.times(1, 1))
                    pe.wait_ge(s_vw[n.par], shifted(n))
                for a_ in range(KPAIR):
                    g_ = 2 * a_ + hf
                    last = mm(banks[BK_PV][VW * g_:VW * (g_ + 1), :].rearrange("p (i q) -> p i q", q=P)[:, :, BLK * b2:BLK * (b2 + 1)],
                              vv[:, n.par, 1 - b2, g_, :], pt[i % 2][:, 4 * BLK * a_:4 * BLK * (a_ + 1)], start=True, stop=True)
                last.then_inc(s_pv, 1)

            def qktr(t, j, i):
                u = TR_USE[i]
                free(t, j, USES[u])
                for a_ in range(4 if i < 2 else KPAIR):
                    if i < 2:
                        p_ = 4 * i + a_
                        src = qs[:, 2 * p_:2 * p_ + 2, :].rearrange("p a b -> p (a b)")
                    else:
                        src = ks[:, 2 * a_:2 * a_ + 2, :].rearrange("p a b -> p (a b)")
                    last = tr(ring(u)[:, P * a_:P * (a_ + 1)], src, ident)
                last.then_inc(s_qktr, 1)

            def wmat(at, n_):
                return w_hi[:, at:at + n_], w_lo[:, at:at + n_]

            def three(bank, whi, wlo, rhi, rlo, start, stop):
                mm(bank, whi, rhi, start=start, stop=False)
                mm(bank, whi, rlo, start=False, stop=False)
                return mm(bank, wlo, rhi, start=False, stop=stop)

            def gate_up(ci, i):
                nn = ci * NF + i
                for which, bank, sf, sd in ((0, BK_G, s_sl, s_g), (1, BK_U, s_a, s_u)):
                    pe.wait_ge(sf, nn + 1)
                    for k in range(KD):
                        whi, wlo = wmat(i % NF * GU + (2 * k + which) * F, F)
                        at = bass.ds(ci * CH + i // NF * CH, CH)
                        last = three(banks[bank + i % 2][:], whi, wlo, h2_hi[:, k, at], h2_lo[:, k, at], k == 0, k == KD - 1)
                    last.then_inc(sd, 1)

            def down(ci, i):
                nn = ci * NF + i
                pe.wait_ge(s_alo, nn + 1)
                if i % NF == 0:
                    pe.wait_ge(s_yt, ci * 2 + (2 + 2 * (i // NF)))
                for k in range(KD):
                    whi, wlo = wmat(DOWN0 + i % NF * D + P * k, P)
                    last = three(banks[BK_Y + k][:], whi, wlo, a_hi[i % 2], a_lo[i % 2], i % NF == 0, i == NF - 1)
                last.then_inc(s_afree, 1)

            def weight_rows(half):
                pe.wait_ge(s_r, routing_steps[half])
                for q in range(HT):
                    last = tr(banks[BK_ROUTE[half][q // 4]][0:NE, P * (q % 4):P * (q % 4 + 1)], r_bufs[:, 4 * HW + NE * q:4 * HW + NE * (q + 1)], ident)
                last.then_inc(s_wtr, 1)

            def chunk(ci, last, second_half):
                for i in range(2, NF):
                    if i + 1 < NF or not last:
                        gate_up(ci, i + 1)
                    down(ci, i - 1)
                    if second_half and i == 12:
                        weight_rows(1)
                if second_half:
                    pe.wait_ge(s_wt, 4)
                if not last:
                    gate_up(ci, NF + 1)
                down(ci, NF - 1)
                if not last:
                    gate_up(ci, NF + 2)
                finish(ci)
                if not last:
                    down(ci, NF)

            def finish(ci):
                for pr in range(2):
                    pe.wait_ge(s_yt, ci * 2 + 4)
                    if pr == 0:
                        pe.wait_ge(s_fin, ci * 2 + 2)
                    for tt in range(2):
                        for k in range(KD):
                            c0 = (2 * pr + tt) * P
                            last = tr(banks[BK_YT + pr][:, D * tt + P * k:D * tt + P * (k + 1)], yt[:, k, c0:c0 + P], ident)
                    last.then_inc(s_ytr, 1)

            pe.sem_inc(s_afree, 2)

            def body(t, j):
                b_, c_, d_, f_ = t + (-1), t + (-2), t + (-3), t + (-4)
                if live(j, 1):
                    pe.wait_ge(s_xn, b_.times(1, 1))
                    for k in range(KD):
                        last = tr(banks[BK_T][:, P * k:P * (k + 1)], xn[:, P * k:P * (k + 1)], ident)
                    last.then_inc(s_xtr, 1)
                if live(j, 2):
                    maxpass(t, j, (0, 1))
                if live(j, 4):
                    pe.wait_ge(s_att, f_.times(1, 1))
                    for k in range(KD):
                        last = mm(banks[BK_PV][:, 0:D], attnt[:, P * k:P * (k + 1)], wo_s[:, k, :], start=(k == 0), stop=(k == KD - 1))
                    last.then_inc(s_wo, 1)
                if j == NT + LAST - 1:
                    pe.wait_ge(s_h2lo, TPC)
                    pe.wait_ge(s_v, NT)
                    pe.wait_ge(s_wlo, NT)
                    gate_up(0, 0)
                if live(j, 1):
                    pe.wait_ge(s_xnt, b_.times(1, 1))
                    if after(j, 1):
                        pe.wait_ge(s_v, b_.times(1))
                        pe.wait_ge(s_ra, b_.times(2))
                    for k in range(KD):
                        last = mm(banks[BK_PROJ][:, 0:QKV], xnt[:, b_.par, k, :], wqkv_s[:, k, :], start=(k == 0), stop=(k == KD - 1))
                    last.then_inc(s_proj, 1)
                if live(j, 3):
                    if j == NT + 2:
                        pe.wait_ge(s_mxr, 8 * NT)
                    tpass(t, j, 0)
                    tpass(t, j, 1)
                if live(j, 2):
                    maxpass(t, j, (2,))
                if live(j, 3):
                    if after(j, 3):
                        pe.wait_ge(s_x1, d_.times(1))
                    values(d_, 0)
                    tpass(t, j, 2)
                if live(j, 2):
                    maxpass(t, j, (3,))
                if live(j, 3):
                    values(d_, 1)
                    tpass(t, j, 3)
                if live(j, 2):
                    maxpass(t, j, (4, 5))
                if live(j, 4):
                    pe.wait_ge(s_z2, f_.times(1, 1))
                    for k in range(KD):
                        last = tr(banks[BK_T][:, P * k:P * (k + 1)], z2[:, P * k:P * (k + 1)], ident)
                    last.then_inc(s_z2tr, 1)
                if live(j, 3):
                    values(d_, 2)
                if live(j, 2):
                    maxpass(t, j, (6, 7))
                if live(j, 3):
                    values(d_, 3)
                if live(j, 1):
                    pe.wait_ge(s_qklo, b_.times(2, 2))
                    if j == 1:
                        pe.wait_ge(s_su, COPY_STEPS)
                    for i in range(2):
                        qktr(t, j, i)
                if live(j, 3):
                    pe.wait_ge(s_ot, d_.times(1, 1))
                    for i in range(4):
                        last = tr(banks[BK_PV][:, P * i:P * (i + 1)], ot[:, P * i:P * (i + 1)], ident)
                    last.then_inc(s_on, 1)
                if live(j, 2):
                    pe.wait_ge(s_ms, c_.times(2, 2))
                    if after(j, 4):
                        pe.wait_ge(s_lgr, f_.times(1))
                    tr(banks[BK_S][0:4 * NPAIR, 0:P], ms[:].rearrange("p a b c -> p (a b c)"), ident).then_inc(s_mtr, 1)
                if live(j, 1):
                    qktr(t, j, 2)
                if j == NT + LAST - 1:
                    gate_up(0, 1)
                    weight_rows(0)
                if live(j, 4):
                    if live(j, 2):
                        pe.wait_ge(s_mt, c_.times(1, 1))
                    pe.wait_ge(s_h32, f_.times(2, 2))
                    for k in range(KD):
                        last = mm(banks[BK_S][:, 0:NE], h32[:, P * k:P * (k + 1)], gw_s[:, k, :], start=(k == 0), stop=(k == KD - 1))
                    last.then_inc(s_lg, 1)

                if live(j, 3):
                    if live(j, 1):
                        pe.wait_ge(s_v, b_.times(1, 1))
                    pe.wait_ge(s_at, d_.times(1, 1))
                    for k in range(KD):
                        last = tr(banks[BK_PROJ][:, P * k:P * (k + 1)], attn[:, P * k:P * (k + 1)], ident)
                    last.then_inc(s_atr, 1)

            turns(pe, body)

            gate_up(0, 2)
            pe.wait_ge(s_wt, 2)
            down(0, 0)
            pe.wait_ge(s_h2lo, NT)
            chunk(0, False, True)
            with pe.Fori(1, NC - 1) as ci:
                chunk(ci, False, False)
            chunk(NC - 1, True, False)


def _consts():
    import numpy as np
    cf = np.zeros((P, NCF), np.float32)
    cf[:, C_ID:C_ID + P] = np.eye(P)
    inv = (1.0 / 10000.0 ** (np.arange(0, HD, 2) / HD)).astype(np.float32)
    ang = np.arange(S, dtype=np.float32)[:, None] * inv[None, :]
    cos, sin = np.cos(ang.astype(np.float64)), np.sin(ang.astype(np.float64))
    c2 = np.repeat(cos, 2, axis=1).reshape(NT, P, HD).transpose(1, 0, 2)
    s2 = np.stack([-sin, sin], axis=-1).reshape(NT, P, HD).transpose(1, 0, 2)
    cf[:, C_COS:C_COS + NT * HD] = c2.reshape(P, -1)
    cf[:, C_SIN:C_SIN + NT * HD] = s2.reshape(P, -1)
    a = np.arange(NGRP)
    cf[:, C_TRI:C_TRI + 16] = (a[None, :] < a[:, None]).astype(np.float32).reshape(1, 16)
    cf[:, C_NHALF] = -0.5
    cb = np.zeros((P, NCB), np.float32)
    cb[:, B_ID:B_ID + P] = np.eye(P)
    i, j = np.arange(P)[:, None], np.arange(KEYS)[None, :]
    ok = (j >= i) & (j <= i + WINDOW)
    cb[:, B_MQ:B_MQ + KEYS] = np.where(ok, 0, NEG)
    cb[:, B_MQ0:B_MQ0 + KEYS] = np.where(ok & (j >= WINDOW), 0, NEG)
    kk, q = np.arange(P)[:, None], np.arange(BLK)[None, :]
    ok = (kk >= q) & (kk <= q + WINDOW)
    cb[:, B_MT:B_MT + BLK] = np.where(ok, 0, NEG)
    cb[:, B_MT0:B_MT0 + BLK] = np.where(ok & (kk >= BLK), 0, NEG)
    return cf, cb


def kernel(L0_attn_x, L0_attn_rms_w, L0_attn_wq, L0_attn_wk, L0_attn_wv, L0_attn_wo, L0_ffn_gate_weight,
           L0_ffn_e_score_correction_bias, L0_ffn_gate_w, L0_ffn_up_w, L0_ffn_down_w, L0_ffn_sh_gate_w,
           L0_ffn_sh_up_w, L0_ffn_sh_down_w, L0_c, L0_wmod):
    import numpy as np
    import concourse.bacc as bacc
    from concourse.bass_utils import run_bass_kernel_spmd

    A = np.asarray
    gw = np.concatenate([A(L0_ffn_sh_gate_w).reshape(2, F, D), A(L0_ffn_gate_w)])
    uw = np.concatenate([A(L0_ffn_sh_up_w).reshape(2, F, D), A(L0_ffn_up_w)])
    gu = np.stack([gw, uw]).reshape(2, NF, F, KD, P).transpose(4, 1, 3, 0, 2).reshape(P, NF * GU)
    dw = np.concatenate([A(L0_ffn_sh_down_w).reshape(D, 2, F).transpose(1, 0, 2), A(L0_ffn_down_w)])
    dn = dw.transpose(2, 0, 1).reshape(P, NF * D)
    wbig = np.concatenate([gu, dn], axis=1).reshape(P, NT, WCH).transpose(1, 0, 2)
    heads = np.arange(NH).reshape(2, NPAIR).T.reshape(-1)
    kv = np.arange(NKV).reshape(2, KPAIR).T.reshape(-1)
    wq, wk, wv = (A(w).reshape(D, -1, HD)[:, o].reshape(D, -1)
                  for w, o in ((L0_attn_wq, heads), (L0_attn_wk, kv), (L0_attn_wv, kv)))
    back = np.array([8 * (g % 2) + 4 * (g // 2) + i for i in range(4) for g in range(NKV)])
    wo = A(L0_attn_wo).reshape(NH, HD, D)[back].reshape(D, D)
    cf, cb = _consts()
    arrays = {
        "x": A(L0_attn_x).reshape(S, D),
        "wqkv": np.concatenate([wq, wk, wv], axis=1),
        "wo": wo, "rms_w": A(L0_attn_rms_w).reshape(KD, P).T, "gate_weight": A(L0_ffn_gate_weight).T,
        "bias": A(L0_ffn_e_score_correction_bias), "wbig": wbig, "c": A(L0_c).reshape(KD, P).T, "wmod": A(L0_wmod),
        "cf": cf, "cb": cb,
    }
    nc = bacc.Bacc("TRN2", target_bir_lowering=False, num_devices=1)
    ins, args = {}, []
    for name, a in arrays.items():
        a = np.ascontiguousarray(a)
        ins[f"in_{name}"] = a
        args.append(nc.dram_tensor(f"in_{name}", a.shape, mybir.dt.from_np(a.dtype), kind="ExternalInput").ap())
    args.append(nc.dram_tensor("out_0", (S, D), F32, kind="ExternalOutput").ap())
    build(nc, *args)
    r = run_bass_kernel_spmd(nc, [ins], core_ids=[0])
    return r.results[0]["out_0"].reshape(1, S, D)
```
